# Optimizing a Trainium2 kernel written in Bass

```python
import numpy as np
import jax
import jax.numpy as jnp

def _softmax(x, axis=-1):
    return jax.nn.softmax(x, axis=axis)

def _gelu(x):
    return jax.nn.gelu(x, approximate=True)

def _silu(x):
    return jax.nn.silu(x)

def _sigmoid(x):
    return jax.nn.sigmoid(x)

def _layernorm(x, axis=-1, eps=1e-05):
    m = jnp.mean(x, axis=axis, keepdims=True)
    v = jnp.var(x, axis=axis, keepdims=True)
    return (x - m) / jnp.sqrt(v + eps)

def _scatter_add(tgt, idx, src, axis=0):
    return tgt.at[idx].add(src)

def _segment_sum(src, seg, n):
    return jax.ops.segment_sum(src, seg, n)
kernel_name = 'mk_seq_postln_d1_jaxref_r8_cfdfb7'

def setup_inputs(seed: int=0):
    np.random.seed(seed)
    _w = jnp.asarray

    def _L0_attn_setup():
        import jax, jax.numpy as jnp
        import numpy as np
        B, T, D, H, NT = (2, 256, 128, 16, 7)
        HD = D // H
        TEMP = 0.5
        key = jax.random.key(seed)
        ks = jax.random.split(key, 6)
        x = jax.random.normal(ks[0], (B, T, D), jnp.float32)
        qkv_w = jax.random.normal(ks[1], (3 * D, D), jnp.float32) / np.sqrt(D)
        out_w = jax.random.normal(ks[2], (D, D), jnp.float32) / np.sqrt(D)
        hex_w = jax.random.normal(ks[3], (6, D), jnp.float32) * 0.02
        q6_w = jax.random.normal(ks[4], (6, D), jnp.float32) * 0.02
        tr = np.zeros((NT, 6, 6), dtype=np.float32)
        for i in range(6):
            tr[i] = np.eye(6)
            tr[i, i, i] = -1.0
        tr[6] = -np.eye(6)
        transforms = jnp.asarray(tr)
        transform_weights = jax.random.normal(ks[5], (H, NT), jnp.float32) * 0.01
        hamming_lambda_logit = jnp.asarray(np.log(0.1 / 0.9), jnp.float32)
        scale_logit = jnp.zeros((), jnp.float32)
        sips_alpha = jnp.ones((1,), jnp.float32)
        sips_beta = jnp.full((1,), np.sqrt(HD), jnp.float32)
        return {'x': x, 'qkv_w': qkv_w, 'out_w': out_w, 'hex_w': hex_w, 'hamming_lambda_logit': hamming_lambda_logit, 'q6_w': q6_w, 'transforms': transforms, 'transform_weights': transform_weights, 'scale_logit': scale_logit, 'sips_alpha': sips_alpha, 'sips_beta': sips_beta}
    _L0_attn_in = _L0_attn_setup()

    def _L0_ffn_setup():
        import jax, jax.numpy as jnp
        import numpy as np
        DIM = 128

        def _reference_tuple_inner(x, W_r, W_k, W_v, mu_r, mu_k):
            B, T, C = x.shape
            x_prev = jnp.concatenate([jnp.zeros((B, 1, C), x.dtype), x[:, :-1, :]], axis=1)
            xr = mu_r * x + (1.0 - mu_r) * x_prev
            xk = mu_k * x + (1.0 - mu_k) * x_prev
            r = jax.nn.sigmoid(jnp.einsum('btc,dc->btd', xr, W_r))
            k = jnp.einsum('btc,dc->btd', xk, W_k)
            k_act = jnp.square(jax.nn.relu(k))
            out = r * jnp.einsum('btc,dc->btd', k_act, W_v)
            new_state = x[:, -1, :]
            return (out, new_state)
        key = jax.random.key(seed)
        ks = jax.random.split(key, 6)
        B, T, C = (8, 256, DIM)
        x = jax.random.normal(ks[0], (B, T, C), dtype=jnp.float32)
        s = 1.0 / np.sqrt(C)
        W_r = jax.random.uniform(ks[1], (C, C), jnp.float32, -s, s)
        W_k = jax.random.uniform(ks[2], (C, C), jnp.float32, -s, s)
        W_v = jax.random.uniform(ks[3], (C, C), jnp.float32, -s, s)
        mu_r = jax.random.uniform(ks[4], (C,), jnp.float32)
        mu_k = jax.random.uniform(ks[5], (C,), jnp.float32)
        return {'x': x, 'W_r': W_r, 'W_k': W_k, 'W_v': W_v, 'mu_r': mu_r, 'mu_k': mu_k}
    _L0_ffn_in = _L0_ffn_setup()
    _d = {'L0_attn_x': _L0_attn_in['x'], 'L0_attn_qkv_w': _L0_attn_in['qkv_w'], 'L0_attn_out_w': _L0_attn_in['out_w'], 'L0_attn_hex_w': _L0_attn_in['hex_w'], 'L0_attn_hamming_lambda_logit': _L0_attn_in['hamming_lambda_logit'], 'L0_attn_q6_w': _L0_attn_in['q6_w'], 'L0_attn_transforms': _L0_attn_in['transforms'], 'L0_attn_transform_weights': _L0_attn_in['transform_weights'], 'L0_attn_scale_logit': _L0_attn_in['scale_logit'], 'L0_attn_sips_alpha': _L0_attn_in['sips_alpha'], 'L0_attn_sips_beta': _L0_attn_in['sips_beta'], 'L0_ffn_W_r': _L0_ffn_in['W_r'], 'L0_ffn_W_k': _L0_ffn_in['W_k'], 'L0_ffn_W_v': _L0_ffn_in['W_v'], 'L0_ffn_mu_r': _L0_ffn_in['mu_r'], 'L0_ffn_mu_k': _L0_ffn_in['mu_k']}
    _x0 = _d['L0_attn_x']
    _d['L0_attn_x'] = jax.random.normal(jax.random.fold_in(jax.random.key(seed), 1), (8, 512, 128), dtype=_x0.dtype)
    del _x0
    return _d

def reference(L0_attn_x, L0_attn_qkv_w, L0_attn_out_w, L0_attn_hex_w, L0_attn_hamming_lambda_logit, L0_attn_q6_w, L0_attn_transforms, L0_attn_transform_weights, L0_attn_scale_logit, L0_attn_sips_alpha, L0_attn_sips_beta, L0_ffn_W_r, L0_ffn_W_k, L0_ffn_W_v, L0_ffn_mu_r, L0_ffn_mu_k):

    def _L0_attn_ref(x, qkv_w, out_w, hex_w, hamming_lambda_logit, q6_w, transforms, transform_weights, scale_logit, sips_alpha, sips_beta):
        import jax, jax.numpy as jnp
        import numpy as np
        B, T, D, H, NT = (2, 256, 128, 16, 7)
        HD = D // H
        TEMP = 0.5
        b, t, _ = x.shape
        qkv = (x @ qkv_w.T).reshape(b, t, 3, H, HD)
        q = jnp.transpose(qkv[:, :, 0], (0, 2, 1, 3))
        k = jnp.transpose(qkv[:, :, 1], (0, 2, 1, 3))
        v = jnpp = jnp.transpose(qkv[:, :, 2], (0, 2, 1, 3))
        raw = jnp.einsum('bhid,bhjd->bhij', q, k)
        scores = sips_alpha[0] * jnp.tanh(raw / sips_beta[0])
        soft_bits = jnp.tanh(x @ hex_w.T)
        hamming = jnp.einsum('bid,bjd->bij', soft_bits, soft_bits) / 2.0
        lam = jax.nn.sigmoid(hamming_lambda_logit)
        scores = scores + lam * hamming[:, None, :, :]
        hexc = jnp.tanh(x @ q6_w.T)
        w = jax.nn.softmax(transform_weights / TEMP, axis=-1)
        Mh = jnp.einsum('ht,tde->hde', w, transforms)
        lat = jnp.einsum('bid,hde,bje->bhij', hexc, Mh, hexc) / 6.0
        lat = lat * (jax.nn.sigmoid(scale_logit) * 2.0)
        scores = scores + lat
        causal = jnp.tril(jnp.ones((t, t), bool))
        scores = jnp.where(causal[None, None], scores, -jnp.inf)
        attn = jax.nn.softmax(scores, axis=-1)
        out = jnp.einsum('bhij,bhjd->bhid', attn, v)
        out = jnp.transpose(out, (0, 2, 1, 3)).reshape(b, t, D)
        return out @ out_w.T

    def _L0_ffn_ref(x, W_r, W_k, W_v, mu_r, mu_k):
        import jax, jax.numpy as jnp
        import numpy as np
        DIM = 128

        def _reference_tuple_inner(x, W_r, W_k, W_v, mu_r, mu_k):
            B, T, C = x.shape
            x_prev = jnp.concatenate([jnp.zeros((B, 1, C), x.dtype), x[:, :-1, :]], axis=1)
            xr = mu_r * x + (1.0 - mu_r) * x_prev
            xk = mu_k * x + (1.0 - mu_k) * x_prev
            r = jax.nn.sigmoid(jnp.einsum('btc,dc->btd', xr, W_r))
            k = jnp.einsum('btc,dc->btd', xk, W_k)
            k_act = jnp.square(jax.nn.relu(k))
            out = r * jnp.einsum('btc,dc->btd', k_act, W_v)
            new_state = x[:, -1, :]
            return (out, new_state)
        return _reference_tuple_inner(x, W_r, W_k, W_v, mu_r, mu_k)[0]
    x = L0_attn_x
    x = _layernorm(x + _L0_attn_ref(x, L0_attn_qkv_w, L0_attn_out_w, L0_attn_hex_w, L0_attn_hamming_lambda_logit, L0_attn_q6_w, L0_attn_transforms, L0_attn_transform_weights, L0_attn_scale_logit, L0_attn_sips_alpha, L0_attn_sips_beta), axis=-1)
    x = _layernorm(x + _L0_ffn_ref(x, L0_ffn_W_r, L0_ffn_W_k, L0_ffn_W_v, L0_ffn_mu_r, L0_ffn_mu_k), axis=-1)
    return x

_drawn_inputs = setup_inputs


def setup_inputs(seed=0):
    import zlib

    import numpy as np

    out = dict(_drawn_inputs(seed))
    spreads = {}
    factors = {'L0_attn_hex_w': 42.335,
     'L0_attn_q6_w': 8.0,
     'L0_attn_transforms': 8.0,
     'L0_attn_transform_weights': 27.211,
     'L0_ffn_W_r': 3.172,
     'L0_ffn_mu_r': 6.281}
    for name, (base, spread) in spreads.items():
        noise = np.random.default_rng([zlib.crc32(name.encode()), seed]).standard_normal(out[name].shape)
        drawn = base * np.exp(spread * noise) if base else spread * noise
        out[name] = jnp.asarray(drawn.astype(out[name].dtype))
    for name, factor in factors.items():
        out[name] = (out[name] * factor).astype(out[name].dtype)
    return out
```

```python
from contextlib import ExitStack

import concourse.bass as bass
from concourse import mybir
from concourse.alu_op_type import AluOpType as ALU

ACT = mybir.ActivationFunctionType
AX = mybir.AxisListType
F32 = mybir.dt.float32
BF16 = mybir.dt.bfloat16

DVE0_TWMAX = 8
DVE0_TW = 10
DVE0_WEIGHTS = 18
DVE0_TWT = 24
DVE0_ABS = 26
DVE0_END = 35

P = 128
LEVELS = 3
LN_EPS = 1e-5
TEMP = 0.5

QUADS = 4
PAIRS_PER_QUAD = 5
PAIRS = QUADS * PAIRS_PER_QUAD
CHUNKS_PER_QUAD = 3
CHUNKS = QUADS * CHUNKS_PER_QUAD
CHUNK_PAIRS = [[0, 1], [2, 3], [4]]
CHUNK_BUFFERS = 4
Q, K, G, J = range(4)

PREP_UNITS = {1: ["xT"], 2: ["q"], 3: ["k"], 4: ["F"], 5: ["v"], 6: ["G"]}
POST_UNITS = {5: ["oT0", "oT1"], 7: ["aT"], 8: ["y"], 11: ["x1T"], 14: ["kk", "rr"], 16: ["kv"]}
ACT_UNITS = {"xT", "q", "k", "F", "kk", "rr"}


def period_uses(post, prep, main=True):
    uses = []
    for t in range(PAIRS):
        uses += [(t, 0), (t, 1)] if main else []
        uses += PREP_UNITS.get(t, []) if prep else []
        uses += POST_UNITS.get(t, []) if post else []
    return uses


class Ring:

    def __init__(self, batches):
        self.last = batches - 1
        self.prologue = period_uses(False, True, False)
        self.first = period_uses(False, True)
        self.steady = period_uses(True, True)
        self.end = period_uses(True, False)
        self.epilogue = period_uses(True, False, False)
        assert all(len(u) % 2 == 0 for u in (self.prologue, self.first, self.steady))

    def uses(self, b):
        if not isinstance(b, int):
            return self.steady
        return {-1: self.prologue, 0: self.first, self.last: self.end,
                self.last + 1: self.epilogue}.get(b, self.steady)

    @staticmethod
    def of(uses, act):
        return sum((u in ACT_UNITS) == act for u in uses)

    def start(self, b, act):
        if isinstance(b, int) and b < 1:
            return 0 if b < 0 else self.of(self.prologue, act)
        if isinstance(b, int) and b > self.last:
            return self.start(self.last, act) + self.of(self.end, act)
        return (b - 1) * self.of(self.steady, act) + self.of(self.prologue + self.first, act)

    def place(self, b, use):
        return self.uses(b).index(use)

    def through(self, b, use):
        act = use in ACT_UNITS
        return self.start(b, act) + self.of(self.uses(b)[:self.place(b, use) + 1], act)


def build(nc, x, qkv_w, out_w, hex_w, lam_logit, q6_w, transforms, transform_weights, scale_logit,
          alpha, beta, w_r, w_k, w_v, mu_r, mu_k, out):
    B, T, D = x.shape
    H, NT = transform_weights.shape
    NB = hex_w.shape[0]
    HD = D // H
    JB = T // P
    assert D == P and H == 4 * QUADS and JB == 4 and B % 2 == 0
    QK_ROWS = LEVELS * LEVELS * HD
    LAT_ROWS = LEVELS * LEVELS * NB
    SHIFT_ROW = 2 * LAT_ROWS
    BIAS_ROWS = SHIFT_ROW + LEVELS
    HEX_J, HEX_I = 32, 96
    NP = HD * 2

    ring = Ring(B)

    with ExitStack() as ctx:
        def sb(name, shape, dt=F32):
            return ctx.enter_context(nc.sbuf_tensor(name, shape, dt))

        def sem(name):
            return ctx.enter_context(nc.semaphore(name))

        raw = ctx.enter_context(nc.psum_tensor("raw", [P, 2, 1024], F32))
        bias = ctx.enter_context(nc.psum_tensor("bias", [P, 2, 512], F32))
        sums = ctx.enter_context(nc.psum_tensor("sums", [P, 2, 512], F32))

        ident = sb("ident", [P, P])
        wqT = sb("wqT", [P, P])
        wkT = sb("wkT", [P, P])
        wvT = sb("wvT", [P, P])
        woT = sb("woT", [P, P])
        w_rT = sb("w_rT", [P, P])
        w_kT = sb("w_kT", [P, P])
        w_vT = sb("w_vT", [P, P])
        w_fT = sb("w_fT", [P, P])
        lat_map = sb("lat_map", [P, P])
        scal = sb("scal", [P, 4])
        tanhs = sb("tanhs", [P, 2])
        cols = sb("cols", [P, 8])
        mu = sb("mu", [P, 2])
        tr_sb = sb("tr_sb", [NT, NB * NB])
        tw = sb("tw", [H, NT])
        tw_max = sb("tw_max", [H, 1])
        tw_exp = sb("tw_exp", [H, NT])
        tw_sum = sb("tw_sum", [H, 1])
        tw_inv = sb("tw_inv", [H, 1])
        twT = sb("twT", [NT, H])
        lat_abs = sb("lat_abs", [NB, H])
        shift_col = sb("shift_col", [P, LEVELS, 1], BF16)
        shift_f = sb("shift_f", [P, 2])
        ones_rows = sb("ones_rows", [LEVELS, T], BF16)
        j_scale = sb("j_scale", [P, 1])
        minus_half = sb("minus_half", [P, JB])

        q_stack = [sb(f"q_stack{n}", [QK_ROWS, H * T], BF16) for n in range(2)]
        k_stack = [sb(f"k_stack{n}", [QK_ROWS, H * T], BF16) for n in range(2)]
        i_stack = [sb(f"i_stack{n}", [BIAS_ROWS, H * T], BF16) for n in range(2)]
        j_stack = [sb(f"j_stack{n}", [BIAS_ROWS, T], BF16) for n in range(2)]
        values = [sb(f"values{n}", [P, JB, H, 32]) for n in range(2)]
        probs = sb("probs", [P, CHUNK_BUFFERS, 4, T])
        w_nat = probs[:, 3, 0:2, :].rearrange("p u (n c) -> p (u n) c", c=P)
        wo_perm = probs[:, 3, 2, 0:P]
        ones = probs[:, 3, 3, :]
        shift_rows = probs[0:H, 2, 0:2, :].rearrange("p u i -> p (u i)").bitcast(BF16)[:, 0:LEVELS * T] \
            .rearrange("p (l i) -> p l i", l=LEVELS)

        x_nat = sb("x_nat", [P, JB, D])
        xT = sb("xT", [P, T])
        feats = sb("feats", [P, T])
        whole = sb("whole", [P, 4, T])
        parts = sb("parts", [P, 4, LEVELS, T], BF16)

        x_res = sb("x_res", [P, JB, D])
        sums_sb = sb("sums_sb", [P, 2, T])
        den_inv = sb("den_inv", [P, 2, JB, H // 2])
        attnT = sb("attnT", [P, T])
        res = sb("res", [P, JB, D])
        bn = sb("bn", [P, JB, 6])
        mean_var = sb("mean_var", [P, JB, 2])
        var_eps = sb("var_eps", [P, JB])
        rstd = sb("rstd", [P, JB])
        x1 = sb("x1", [P, JB, D])
        attn = x1
        x1T = sb("x1T", [P, 1 + T])
        x_diff = sb("x_diff", [P, T])
        gated = x_diff
        xk = sb("xk", [P, T])
        xr = sb("xr", [P, T])
        k_act = sb("k_act", [P, T])
        r_tanh = sb("r_tanh", [P, JB, D])
        final = sb("final", [P, JB, D])

        scratch = nc.dram_tensor("scratch", [4, LEVELS, P, T], BF16, kind="Internal").ap()
        shift_dram = nc.dram_tensor("shift_dram", [LEVELS, H, T], BF16, kind="Internal").ap()

        s_w, s_small, s_ident, s_zero = sem("w_in"), sem("small_in"), sem("ident_made"), sem("zeroed")
        s_wT, s_wT_out = sem("w_transposed"), sem("w_copied")
        s_pool0 = sem("pool_setup")
        s_tanhs, s_twexp = sem("logit_tanhs"), sem("tw_exp_made")
        s_dve0 = sem("dve_setup")
        s_twT, s_lat, s_bound = sem("tw_transposed"), sem("lattice_product"), sem("bound_product")
        s_twT_out, s_lat_out, s_consts = sem("tw_copied"), sem("lattice_copied"), sem("consts_made")
        s_shift_d, s_const_rows = sem("shift_in_dram"), sem("const_rows_in")
        s_setup_psum = sem("setup_psum_read")

        raw_ready = sem("raw_ready")
        tanh_done = sem("tanh_done")
        dve_unit = sem("dve_unit")
        act_unit = sem("act_unit")
        dve_freed = sem("dve_freed")
        act_freed = sem("act_freed")
        exp_done = sem("exp_done")
        mask_done = sem("mask_done")
        pv_done = sem("pv_done")
        sums_read = sem("sums_read")

        x_in = sem("x_in")
        j_ready = sem("j_ready")
        hi_done, mid_done = sem("hi_done"), sem("mid_done")
        rest_done, lo_done = sem("rest_done"), sem("lo_done")
        scr_in = [sem(f"scratch_in{n}") for n in range(4)]
        STACK_DMAS = [LEVELS, LEVELS, LEVELS + LEVELS * LEVELS, 2 * LEVELS]
        stack_in = [sem(f"stack_in{n}") for n in range(4)]

        xres_in = sem("xres_in")
        den_done, attn_done = sem("den_done"), sem("attn_done")
        res_done = sem("res_done")
        bn_done, aggr_done = sem("bn_done"), sem("aggr_done")
        eps_done, rstd_done = sem("eps_done"), sem("rstd_done")
        norm_done = sem("norm_done")
        diff_done = sem("diff_done")
        xk_done, xr_done = sem("xk_done"), sem("xr_done")
        kact_done = sem("kact_done")
        gate_done = sem("gate_done")
        stored = sem("stored")

        passed = sem("passed")

        block = ctx.enter_context(nc.Block())

        def pair_units(t):
            quad, p = divmod(t, PAIRS_PER_QUAD)
            if p < 2:
                return [[(4 * quad + r, 0, 0, T)] for r in (2 * p, 2 * p + 1)]
            if p < 4:
                return [[(4 * quad + r, 1, 0, 3 * P), (4 * quad + r, 3, 3 * P, P)] for r in (2 * p - 4, 2 * p - 3)]
            return [[(4 * quad + r, 2, (r % 2) * 2 * P, 2 * P) for r in (2 * u, 2 * u + 1)] for u in range(2)]

        def chunk_of(t):
            quad, p = divmod(t, PAIRS_PER_QUAD)
            return quad * CHUNKS_PER_QUAD + p // 2

        def last_pair(c):
            quad, i = divmod(c, CHUNKS_PER_QUAD)
            return quad * PAIRS_PER_QUAD + CHUNK_PAIRS[i][-1]

        def pair_probs(t):
            c = chunk_of(t)
            at = (t - (last_pair(c - 1) + 1 if c else 0)) * 2
            return probs[:, c % CHUNK_BUFFERS, at:at + 2, :]

        CHUNK_END = {last_pair(c): c for c in range(CHUNKS)}

        def stand_alone(eng):
            eng.sem_inc(passed, 1)

        @block.sync
        def _(sp):
            sp.dma_start(x_nat[:], x[0].rearrange("(n p) c -> p n c", p=P)).then_inc(x_in, 16)
            sp.dma_start(w_nat[:, 0:3, :], qkv_w.rearrange("(t p) c -> p t c", p=P)).then_inc(s_w, 16)
            for n, w in enumerate((out_w, w_r, w_k, w_v)):
                sp.dma_start(w_nat[:, 3 + n, :], w).then_inc(s_w, 16)
            sp.wait_ge(s_zero, 1)
            sp.dma_start(w_nat[0:NB, 7, :], q6_w).then_inc(s_w, 16)
            sp.dma_start(w_nat[HEX_J:HEX_J + NB, 7, :], hex_w).then_inc(s_w, 16)
            sp.dma_start(w_nat[HEX_I:HEX_I + NB, 7, :], hex_w).then_inc(s_w, 16)
            for n, s in enumerate((lam_logit, scale_logit, alpha, beta)):
                sp.dma_start(scal[:, n:n + 1], s.partition_broadcast(P)).then_inc(s_small, 16)
            sp.dma_start(mu[:, 0:1], mu_r.rearrange("(p a) -> p a", a=1)).then_inc(s_small, 16)
            sp.dma_start(mu[:, 1:2], mu_k.rearrange("(p a) -> p a", a=1)).then_inc(s_small, 16)
            sp.dma_start(tr_sb[:], transforms.rearrange("t d e -> t (d e)")).then_inc(s_small, 16)
            sp.dma_start(tw[:], transform_weights).then_inc(s_small, 16)

            sp.wait_ge(s_consts, 1)
            sp.dma_start(shift_dram.rearrange("l h i -> h l i"), shift_rows).then_inc(s_shift_d, 16)
            sp.wait_ge(s_shift_d, 16)
            for n in range(2):
                sp.dma_start(i_stack[n][SHIFT_ROW:BIAS_ROWS, :],
                             shift_dram.rearrange("l h i -> l (h i)")).then_inc(s_const_rows, 16)
                sp.dma_start(j_stack[n][SHIFT_ROW:BIAS_ROWS, :], ones_rows[:]).then_inc(s_const_rows, 16)

            def stacks(n, par):
                early = isinstance(n, int) and n == 0
                for kind in (Q, K, G, J):
                    sp.wait_ge(lo_done, 4 * n + kind + 1)
                    stand_alone(sp)
                    if not early:
                        sp.wait_ge(stack_in[kind], 16 * STACK_DMAS[kind] * n)
                    sp.dma_start(scratch[kind].rearrange("l p i -> p l i"),
                                 parts[:, kind]).then_inc(scr_in[kind], 16)
                if not (isinstance(n, int) and n < 2):
                    sp.wait_ge(raw_ready, PAIRS * (n - 1))
                    sp.wait_ge(dve_unit, ring.start(n - 1, False))
                for kind in (Q, K, G, J):
                    sp.wait_ge(scr_in[kind], 16 * (n + 1))
                    load_stack(kind, par)

            def load_stack(kind, par):
                ready = stack_in[kind]
                for lk in range(LEVELS):
                    r = lk * LEVELS * HD
                    if kind == Q:
                        sp.dma_start(q_stack[par][r:r + LEVELS * HD, :],
                                     scratch[Q].rearrange("l (d h) i -> (l d) (h i)", h=H)).then_inc(ready, 16)
                    if kind == K:
                        part = scratch[K, lk].rearrange("(d h) i -> d (h i)", h=H)
                        sp.dma_start(k_stack[par][r:r + LEVELS * HD, :],
                                     part.unsqueeze(0).broadcast_to([LEVELS, HD, H * T])).then_inc(ready, 16)
                for lj in range(LEVELS):
                    r = lj * LEVELS * NB
                    if kind == G:
                        lat = scratch[G][:, 0:NB * H, :].rearrange("l (e h) i -> l e (h i)", h=H)
                        sp.dma_start(i_stack[par][r:r + LEVELS * NB, :], lat).then_inc(ready, 16)
                        for li in range(LEVELS):
                            at = LAT_ROWS + r + li * NB
                            ham = scratch[G, li, HEX_I:HEX_I + NB, :].unsqueeze(1).broadcast_to([NB, H, T])
                            sp.dma_start(i_stack[par][at:at + NB, :].rearrange("e (h i) -> e h i", h=H),
                                         ham).then_inc(ready, 16)
                    if kind == J:
                        for at, row in ((r, 0), (LAT_ROWS + r, HEX_J)):
                            part = scratch[J, lj, row:row + NB, :]
                            sp.dma_start(j_stack[par][at:at + LEVELS * NB, :],
                                         part.unsqueeze(0).broadcast_to([LEVELS, NB, T])).then_inc(ready, 16)

            def period(b, par, post, prep):
                if post:
                    sp.wait_ge(dve_freed, ring.start(b, False))
                    stand_alone(sp)
                    sp.dma_start(x_res[:], x[b - 1].rearrange("(n p) c -> p n c", p=P)).then_inc(xres_in, 16)
                if prep:
                    stacks(b + 1, 1 - par)
                if post:
                    store(b - 1)

            def store(n):
                sp.wait_ge(norm_done, 2 * JB * (n + 1))
                stand_alone(sp)
                sp.dma_start(out[n].rearrange("(n p) c -> p n c", p=P), final[:]).then_inc(stored, 16)
                sp.wait_ge(stored, 16 * (n + 1))
                stand_alone(sp)

            stacks(0, 0)
            period(0, 0, False, True)
            with sp.Fori(1, B - 2, 2) as i:
                period(i, 1, True, True)
                period(i + 1, 0, True, True)
            period(B - 1, 1, True, False)
            sp.wait_ge(dve_freed, ring.start(B - 1, False) + ring.of(ring.end, False))
            sp.dma_start(x_res[:], x[B - 1].rearrange("(n p) c -> p n c", p=P)).then_inc(xres_in, 16)
            store(B - 1)

        @block.tensor
        def _(pe):
            def mm(o, lhsT, rhs, start=True, stop=True, **kw):
                return nc.tensor.matmul(o, lhsT, rhs, start=start, stop=stop, **kw)

            pe.wait_ge(s_ident, 1)
            pe.wait_ge(s_w, 16 * 8)
            pe.wait_ge(s_small, 16 * 8)
            pe.wait_ge(s_zero, 2)
            for n in range(8):
                src = wo_perm if n == 3 else w_nat[:, n, :]
                last = nc.tensor.transpose(raw[:, 0, n * P:(n + 1) * P], src, ident[:])
            last.then_inc(s_wT, 1)
            pe.wait_ge(s_dve0, DVE0_TW)
            nc.tensor.transpose(raw[0:NT, 1, 0:H], tw[:], ident[0:H, 0:H]).then_inc(s_twT, 1)
            pe.wait_ge(s_dve0, DVE0_TWT)
            for e in range(NB):
                last = mm(raw[0:NB, 1, 512 + e * H:512 + (e + 1) * H],
                          tr_sb[:].rearrange("t (d e) -> t d e", e=NB)[:, :, e], twT[:])
            last.then_inc(s_lat, 1)
            pe.wait_ge(s_dve0, DVE0_ABS)
            mm(raw[:, 1, 0:H], ones[0:NB, 0:P], lat_abs[:]).then_inc(s_bound, 1)

            def slot(b, use):
                n = ring.place(b, use)
                if n >= 2:
                    before = ring.uses(b)[n - 2]
                    pe.wait_ge(act_freed if before in ACT_UNITS else dve_freed, ring.through(b, before))
                elif not (isinstance(b, int) and b < 0):
                    pe.wait_ge(dve_freed, ring.start(b, False) - 1 + n)
                return bias[:, n % 2, :]

            def scores(b, par, t):
                if t == 0:
                    pe.wait_ge(stack_in[Q], 16 * STACK_DMAS[Q] * (b + 1))
                    pe.wait_ge(stack_in[K], 16 * STACK_DMAS[K] * (b + 1))
                if isinstance(b, int) and b == 0 and t < 2:
                    pe.wait_ge(s_dve0, DVE0_END)
                else:
                    pe.wait_ge(tanh_done, PAIRS * b + t - 1)
                for u, bank in enumerate(pair_units(t)):
                    for h, jb, at, n in bank:
                        last = mm(raw[:, t % 2, 512 * u + at:512 * u + at + n],
                                  k_stack[par][:, h * T + jb * P:h * T + (jb + 1) * P],
                                  q_stack[par][:, h * T + jb * P:(h + 1) * T])
                last.then_inc(raw_ready, 1)

            def biases(b, par, t):
                if t == 0:
                    pe.wait_ge(stack_in[G], 16 * STACK_DMAS[G] * (b + 1))
                    pe.wait_ge(stack_in[J], 16 * STACK_DMAS[J] * (b + 1))
                for u, bank in enumerate(pair_units(t)):
                    o = slot(b, (t, u))
                    for h, jb, at, n in bank:
                        last = mm(o[:, at:at + n], j_stack[par][:, jb * P:(jb + 1) * P],
                                  i_stack[par][:, h * T + jb * P:(h + 1) * T])
                    last.then_inc(dve_unit, 1)

            def weighted(b, par, c):
                quad, i = divmod(c, CHUNKS_PER_QUAD)
                k, s = divmod(quad, 2)
                pe.wait_ge(mask_done, CHUNKS * b + c + 1)
                if c == 0:
                    pe.wait_ge(dve_freed, ring.through(b - 1, "v"))
                if c in (0, CHUNKS // 2) and not (isinstance(b, int) and b == 0):
                    pe.wait_ge(sums_read, 2 * b - 1 + k)
                buf = probs[:, c % CHUNK_BUFFERS]
                blocks = {0: [(0, 0, T)], 1: [(1, 0, 3 * P), (3, 3 * P, P)], 2: [(2, None, 2 * P)]}[i]
                for jb, at, n in blocks:
                    for r in range(4):
                        rhs = buf[:, r, at:at + n] if at is not None else \
                            buf[:, r // 2, (r % 2) * n:(r % 2 + 1) * n]
                        last = mm(sums[32 * r:32 * r + 32, k, jb * P:T],
                                  values[par][:, jb, 4 * quad + r, :], rhs,
                                  start=(s == 0 and i == 0), stop=(s == 1 and i == 2), skip_group_check=True)
                last.then_inc(pv_done, 1)

            def four(o, lhsT, rhs):
                for n in range(JB):
                    last = mm(o[:, n * P:(n + 1) * P], lhsT[:, n * P:(n + 1) * P], rhs)
                return last

            def four_transposes(o, src):
                for n in range(JB):
                    last = nc.tensor.transpose(o[:, n * P:(n + 1) * P], src(n), ident[:])
                return last

            def side(b, use):
                nx, pv = b + 1, b - 1
                o = slot(b, use)
                done = act_unit if use in ACT_UNITS else dve_unit
                if use == "xT":
                    pe.wait_ge(x_in, 16 * (nx + 1))
                    last = four_transposes(o, lambda n: x_nat[:, n, :])
                elif use in ("q", "k"):
                    pe.wait_ge(act_freed, ring.through(b, "xT"))
                    last = mm(o, wqT[:] if use == "q" else wkT[:], xT[:])
                elif use == "F":
                    last = mm(o, w_fT[:], xT[:])
                elif use == "v":
                    last = four(o, xT, wvT[:])
                elif use == "G":
                    pe.wait_ge(act_freed, ring.through(b, "F"))
                    last = mm(o, lat_map[:], feats[:])
                elif use in ("oT0", "oT1"):
                    k = int(use[-1])
                    pe.wait_ge(sums_read, 2 * pv + 1 + k)
                    last = four_transposes(o, lambda n: sums_sb[:, k, n * P:(n + 1) * P])
                elif use == "aT":
                    pe.wait_ge(dve_freed, ring.through(b, "oT1"))
                    last = four_transposes(o, lambda n: attn[:, n, :])
                elif use == "y":
                    pe.wait_ge(dve_freed, ring.through(b, "aT"))
                    last = four(o, attnT, woT[:])
                elif use == "x1T":
                    pe.wait_ge(norm_done, 2 * JB * pv + JB)
                    last = four_transposes(o, lambda n: x1[:, n, :])
                elif use == "kk":
                    pe.wait_ge(xk_done, pv + 1)
                    last = mm(o, w_kT[:], xk[:])
                elif use == "rr":
                    pe.wait_ge(xr_done, pv + 1)
                    last = four(o, xr, w_rT[:])
                elif use == "kv":
                    pe.wait_ge(kact_done, pv + 1)
                    last = four(o, k_act, w_vT[:])
                last.then_inc(done, 1)

            def period(b, par, post, prep):
                for t in range(PAIRS):
                    if t + 1 < PAIRS:
                        scores(b, par, t + 1)
                    elif prep:
                        scores(b + 1, 1 - par, 0)
                    biases(b, par, t)
                    for use in (PREP_UNITS.get(t, []) if prep else []) + (POST_UNITS.get(t, []) if post else []):
                        side(b, use)
                    c = CHUNK_END.get(t)
                    if c is not None and c >= 2:
                        weighted(b, par, c - 2)
                    elif c is not None and post:
                        weighted(b - 1, 1 - par, CHUNKS - 2 + c)

            pe.wait_ge(s_dve0, DVE0_WEIGHTS)
            for use in ring.prologue:
                side(-1, use)
            pe.wait_ge(s_const_rows, 16 * 4)
            scores(0, 0, 0)
            period(0, 0, False, True)
            with pe.Fori(1, B - 2, 2) as i:
                period(i, 1, True, True)
                period(i + 1, 0, True, True)
            period(B - 1, 1, True, False)
            for c in (CHUNKS - 2, CHUNKS - 1):
                weighted(B - 1, 1, c)
            for t in sorted(POST_UNITS):
                for use in POST_UNITS[t]:
                    side(B, use)

        @block.scalar
        def _(act):
            act.wait_ge(s_small, 16 * 8)
            nc.scalar.activation(tanhs[:], scal[:, 0:2], ACT.Tanh, scale=0.5).then_inc(s_tanhs, 1)
            act.wait_ge(s_dve0, DVE0_TWMAX)
            nc.scalar.activation(tw_exp[:], tw[:], ACT.Exp, bias=tw_max[:], scale=1.0 / TEMP,
                                 accum_out=tw_sum[:]).then_inc(s_twexp, 1)

            def tanh(b, t):
                c = chunk_of(t)
                act.wait_ge(raw_ready, PAIRS * b + t + 1)
                if t == 0 or chunk_of(t - 1) != c:
                    if not (isinstance(b, int) and b == 0 and c < CHUNK_BUFFERS):
                        act.wait_ge(pv_done, CHUNKS * b + c - CHUNK_BUFFERS + 1)
                nc.scalar.activation(pair_probs(t), raw[:, t % 2, :].rearrange("p (u i) -> p u i", u=2),
                                     ACT.Tanh).then_inc(tanh_done, 1)

            def exp(b, c):
                act.wait_ge(dve_freed, ring.through(b, (last_pair(c), 1)))
                buf = probs[:, c % CHUNK_BUFFERS, 0:2 * len(CHUNK_PAIRS[c % CHUNKS_PER_QUAD]), :]
                nc.scalar.activation(buf, buf, ACT.Exp).then_inc(exp_done, 1)

            def side(b, use):
                nx, pv = b + 1, b - 1
                early = isinstance(b, int) and b < 0
                o = bias[:, ring.place(b, use) % 2, :]
                act.wait_ge(act_unit, ring.through(b, use))
                if use == "xT":
                    ins = nc.scalar.activation(xT[:], o, ACT.Copy)
                elif use in ("q", "k"):
                    kind = Q if use == "q" else K
                    if early:
                        act.wait_ge(s_dve0, DVE0_END)
                    else:
                        act.wait_ge(lo_done, 4 * (nx - 1) + kind + 1)
                    ins = nc.scalar.activation(whole[:, kind, :], o, ACT.Copy,
                                               scale=cols[:, 2:3] if use == "q" else 1.0)
                elif use == "F":
                    if not early:
                        act.wait_ge(j_ready, nx)
                    ins = nc.scalar.activation(feats[:], o, ACT.Tanh)
                elif use == "kk":
                    ins = nc.scalar.activation(k_act[:], o, ACT.Relu)
                elif use == "rr":
                    ins = nc.scalar.activation(r_tanh[:].rearrange("p n c -> p (n c)"), o, ACT.Tanh, scale=0.5)
                ins.then_inc(act_freed, 1)

            def period(b, par, post, prep):
                if prep:
                    act.wait_ge(act_unit, ring.through(b - 1, "xT"))
                    act.dma_start(x_nat[:], x[b + 1].rearrange("(n p) c -> p n c", p=P)).then_inc(x_in, 16)
                for t in range(PAIRS):
                    tanh(b, t)
                    for use in (PREP_UNITS.get(t - 1, []) if prep else []) + \
                            (POST_UNITS.get(t - 1, []) if post else []):
                        if use in ACT_UNITS:
                            side(b, use)
                    c = CHUNK_END.get(t)
                    if c is not None and c >= 1:
                        exp(b, c - 1)
                    elif c is not None and post:
                        exp(b - 1, CHUNKS - 1)

            for use in ring.prologue:
                if use in ACT_UNITS:
                    side(-1, use)
            period(0, 0, False, True)
            with act.Fori(1, B - 2, 2) as i:
                period(i, 1, True, True)
                period(i + 1, 0, True, True)
            period(B - 1, 1, True, False)
            exp(B - 1, CHUNKS - 1)
            for t in sorted(POST_UNITS):
                for use in POST_UNITS[t]:
                    if use in ACT_UNITS:
                        side(B, use)

        @block.gpsimd
        def _(pool):
            nc.gpsimd.memset(ident[:], 0.0).then_inc(s_pool0, 1)
            pool.wait_ge(s_pool0, 1)
            nc.gpsimd.affine_select(out=ident[:], in_=ident[:], compare_op=ALU.not_equal, fill=1.0, base=0,
                                    pattern=[[-1, P]], channel_multiplier=1).then_inc(s_ident, 1)
            for n in range(2):
                nc.gpsimd.memset(values[n][:], 0.0).then_inc(s_pool0, 1)
            pool.wait_ge(s_pool0, 3)
            for n in range(2):
                for s in range(2):
                    v = values[n][:].rearrange("p j (k s r) m -> p (j k) s r m", k=2, s=2)
                    nc.gpsimd.memset(v[:, :, s, :, NP * s + HD], 1.0).then_inc(s_pool0, 1)

            def mask(b, c):
                buf = probs[:, c % CHUNK_BUFFERS]
                i = c % CHUNKS_PER_QUAD
                blocks = {0: [buf[:, :, 0:P]], 1: [buf[:, :, 0:P], buf[:, :, 3 * P:T]],
                          2: [buf[:, 0:2, :].rearrange("p u (r i) -> p (u r) i", r=2)[:, :, 0:P]]}[i]
                pool.wait_ge(exp_done, CHUNKS * b + c + 1)
                stand_alone(pool)
                for v in blocks:
                    last = nc.gpsimd.affine_select(out=v, in_=v, compare_op=ALU.is_ge, fill=0.0, base=0,
                                                   pattern=[[0, 4], [1, P]], channel_multiplier=-1)
                last.then_inc(mask_done, 1)

            def rest(n, kind):
                pool.wait_ge(hi_done, 4 * n + kind + 1)
                w = whole[:, kind, :]
                nc.gpsimd.tensor_tensor(w, w, parts[:, kind, 0, :], ALU.subtract).then_inc(rest_done, 1)

            def lo(n, kind):
                pool.wait_ge(mid_done, 4 * n + kind + 1)
                nc.gpsimd.tensor_tensor(parts[:, kind, 2, :], whole[:, kind, :], parts[:, kind, 1, :],
                                        ALU.subtract).then_inc(lo_done, 1)

            def inv_std(n, which):
                m = 2 * n + which
                pool.wait_ge(aggr_done, JB * (m + 1))
                stand_alone(pool)
                nc.gpsimd.tensor_scalar(var_eps[:], mean_var[:, :, 1], LN_EPS, None, ALU.add).then_inc(eps_done, 1)
                pool.wait_ge(eps_done, m + 1)
                nc.gpsimd.tensor_tensor(rstd[:], var_eps[:], minus_half[:], ALU.pow).then_inc(rstd_done, 1)

            def difference(n):
                pool.wait_ge(dve_freed, ring.through(n + 1, "x1T"))
                nc.gpsimd.tensor_tensor(x_diff[:], x1T[:, 1:1 + T], x1T[:, 0:T], ALU.subtract).then_inc(diff_done, 1)

            def square(n):
                pool.wait_ge(act_freed, ring.through(n + 1, "kk"))
                nc.gpsimd.tensor_tensor(k_act[:], k_act[:], k_act[:], ALU.mult).then_inc(kact_done, 1)

            PREP = {4: [(rest, Q)], 5: [(rest, K)], 6: [(lo, Q)], 7: [(rest, G), (lo, K), (rest, J)],
                    9: [(lo, G), (lo, J)]}
            POST = {9: [(inv_std, 0)], 12: [(difference,)], 15: [(square,)], 17: [(inv_std, 1)]}

            def period(b, par, post, prep):
                for t in range(PAIRS):
                    c = CHUNK_END.get(t)
                    if c is not None and c >= 1:
                        mask(b, c - 1)
                    elif c is not None and post:
                        mask(b - 1, CHUNKS - 1)
                    for stage, *a in PREP.get(t, []) if prep else []:
                        stage(b + 1, *a)
                    for stage, *a in POST.get(t, []) if post else []:
                        stage(b - 1, *a)

            for t in sorted(PREP):
                for stage, *a in PREP[t]:
                    stage(0, *a)
            period(0, 0, False, True)
            with pool.Fori(1, B - 2, 2) as i:
                period(i, 1, True, True)
                period(i + 1, 0, True, True)
            period(B - 1, 1, True, False)
            mask(B - 1, CHUNKS - 1)
            for t in sorted(POST):
                for stage, *a in POST[t]:
                    stage(B - 1, *a)

        @block.vector
        def _(dve):
            made = [0]

            def link(ins):
                made[0] += 1
                ins.then_inc(s_dve0, 1)
                dve.wait_ge(s_dve0, made[0])

            def mark(value):
                assert made[0] == value, (made[0], value)

            v = nc.vector
            v.memset(w_nat[:, 7, :], 0.0).then_inc(s_zero, 1)
            link(v.memset(ones, 1.0))
            link(v.memset(minus_half[:], -0.5))
            link(v.memset(x1T[:, 0:1], 0.0))
            link(v.memset(lat_map[:], 0.0))
            link(v.memset(j_scale[:], 1.0))
            link(v.memset(ones_rows[:], 1.0))
            dve.wait_ge(s_small, 16 * 8)
            link(v.tensor_reduce(tw_sum[:], tw[:], AX.X, ALU.max))
            link(v.tensor_scalar(tw_max[:], tw_sum[:], -1.0 / TEMP, None, ALU.mult))
            mark(DVE0_TWMAX)
            dve.wait_ge(s_w, 16 * 8)
            for k in range(2):
                for s in range(2):
                    src = w_nat[:, 3, :].rearrange("p (k s r d) -> p k s r d", k=2, s=2, r=4)[:, k, s]
                    dst = wo_perm.rearrange("p (k r s d) -> p k r s d", k=2, s=2, r=4)[:, k, :, s]
                    last = v.tensor_copy(dst, src)
            last.then_inc(s_zero, 1)
            dve.wait_ge(s_twexp, 1)
            link(v.reciprocal(tw_inv[:], tw_sum[:]))
            link(v.tensor_scalar(tw[:], tw_exp[:], tw_inv[:], None, ALU.mult))
            mark(DVE0_TW)
            dve.wait_ge(s_wT, 1)
            for n, w in enumerate((wqT, wkT, wvT, woT, w_rT, w_kT, w_vT, w_fT)):
                src = raw[:, 0, n * P:(n + 1) * P]
                if n < 2:
                    link(v.tensor_copy(w[:].rearrange("p (d h) -> p d h", h=H),
                                       src.rearrange("p (h d) -> p d h", h=H)))
                else:
                    link(v.tensor_copy(w[:], src))
            mark(DVE0_WEIGHTS)
            dve.wait_ge(s_tanhs, 1)
            link(v.tensor_scalar(cols[:, 0:1], tanhs[:, 0:1], 0.25, 0.25, ALU.mult, ALU.add))
            link(v.tensor_scalar(cols[:, 1:2], tanhs[:, 1:2], 1.0 / NB, 1.0 / NB, ALU.mult, ALU.add))
            link(v.reciprocal(cols[:, 2:3], scal[:, 3:4]))
            link(v.tensor_copy(j_scale[HEX_J:HEX_J + NB, :], cols[HEX_J:HEX_J + NB, 0:1]))
            dve.wait_ge(s_ident, 1)
            link(v.tensor_copy(lat_map[HEX_I:P, HEX_I:P], ident[HEX_I:P, HEX_I:P]))
            dve.wait_ge(s_twT, 1)
            link(v.tensor_copy(twT[:], raw[0:NT, 1, 0:H]))
            mark(DVE0_TWT)
            dve.wait_ge(s_lat, 1)
            link(v.tensor_scalar(lat_map[0:NB, 0:NB * H], raw[0:NB, 1, 512:512 + NB * H], cols[0:NB, 1:2], None,
                                 ALU.mult))
            link(v.tensor_reduce(lat_abs[:], lat_map[0:NB, 0:NB * H].rearrange("d (e h) -> d h e", h=H), AX.X,
                                 ALU.add, apply_absolute_value=True))
            mark(DVE0_ABS)
            link(v.scalar_tensor_tensor(out=cols[:, 3:4], in0=scal[:, 2:3], scalar=-1.0, in1=scal[:, 2:3],
                                        op0=ALU.mult, op1=ALU.max))
            link(v.scalar_tensor_tensor(out=cols[:, 4:5], in0=cols[:, 0:1], scalar=float(NB), in1=cols[:, 3:4],
                                        op0=ALU.mult, op1=ALU.add))
            dve.wait_ge(s_bound, 1)
            link(v.tensor_reduce(cols[:, 5:6], raw[:, 1, 0:H], AX.X, ALU.max))
            link(v.scalar_tensor_tensor(out=cols[:, 6:7], in0=cols[:, 4:5], scalar=-1.0, in1=cols[:, 5:6],
                                        op0=ALU.mult, op1=ALU.subtract))
            link(v.tensor_copy(shift_col[:, 0], cols[:, 6:7]))
            link(v.tensor_tensor(shift_f[:, 0:1], cols[:, 6:7], shift_col[:, 0], ALU.subtract))
            link(v.tensor_copy(shift_col[:, 1], shift_f[:, 0:1]))
            link(v.tensor_tensor(shift_f[:, 1:2], shift_f[:, 0:1], shift_col[:, 1], ALU.subtract))
            link(v.tensor_copy(shift_col[:, 2], shift_f[:, 1:2]))
            for l in range(LEVELS):
                last = v.tensor_scalar(shift_rows[:, l, :], ones[0:H, :], shift_col[0:H, l], None, ALU.mult)
            last.then_inc(s_consts, 1)
            mark(DVE0_END)

            def main(b, t):
                dve.wait_ge(tanh_done, PAIRS * b + t + 1)
                for u in range(2):
                    dve.wait_ge(dve_unit, ring.through(b, (t, u)))
                    o = pair_probs(t)[:, u, :]
                    v.scalar_tensor_tensor(out=o, in0=o, scalar=scal[:, 2:3],
                                           in1=bias[:, ring.place(b, (t, u)) % 2, :], op0=ALU.mult,
                                           op1=ALU.add).then_inc(dve_freed, 1)

            def unit(b, use):
                dve.wait_ge(dve_unit, ring.through(b, use))
                return bias[:, ring.place(b, use) % 2, :]

            def hi(n, kind):
                if kind in (Q, K):
                    dve.wait_ge(act_freed, ring.through(n - 1, "qk"[kind]))
                elif kind == G:
                    dve.wait_ge(dve_freed, ring.through(n - 1, "G"))
                else:
                    dve.wait_ge(j_ready, n + 1)
                if not (isinstance(n, int) and n == 0):
                    dve.wait_ge(scr_in[kind], 16 * n)
                v.tensor_copy(parts[:, kind, 0, :], whole[:, kind, :]).then_inc(hi_done, 1)

            def mid(n, kind):
                dve.wait_ge(rest_done, 4 * n + kind + 1)
                v.tensor_copy(parts[:, kind, 1, :], whole[:, kind, :]).then_inc(mid_done, 1)

            def values_in(n, par):
                o = unit(n - 1, "v")
                if isinstance(n, int) and n < 2:
                    dve.wait_ge(s_pool0, 3 + 4)
                else:
                    dve.wait_ge(pv_done, CHUNKS * (n - 1))
                for s in range(2):
                    dst = values[par][:].rearrange("p j (k s r) m -> p (j k) s r m", k=2, s=2)
                    src = o.rearrange("p (j s r d) -> p j s r d", s=2, r=4, d=HD)
                    last = v.tensor_copy(dst[:, :, s, :, NP * s:NP * s + HD], src[:, :, s])
                last.then_inc(dve_freed, 1)

            def features(n):
                o = unit(n - 1, "G")
                if not (isinstance(n, int) and n == 0):
                    dve.wait_ge(lo_done, 4 * n)
                v.tensor_copy(whole[:, G, :], o).then_inc(dve_freed, 1)
                dve.wait_ge(act_freed, ring.through(n - 1, "F"))
                v.tensor_scalar(whole[:, J, :], feats[:], j_scale[:], None, ALU.mult).then_inc(j_ready, 1)

            def sums_out(n):
                dve.wait_ge(pv_done, CHUNKS * (n + 1))
                for k in range(2):
                    v.tensor_copy(sums_sb[:, k, :], sums[:, k, :]).then_inc(sums_read, 1)

            def normalise(n, k):
                o = unit(n + 1, f"oT{k}").rearrange("p (n q m) -> p n q m", n=JB, m=NP)
                v.reciprocal(den_inv[:, k], o[:, :, :, HD]).then_inc(den_done, 1)
                dve.wait_ge(den_done, 2 * n + k + 1)
                dst = attn[:].rearrange("p n (k q d) -> p n k q d", k=2, d=HD)[:, :, k]
                v.tensor_tensor(dst, o[:, :, :, 0:HD],
                                den_inv[:, k].unsqueeze(3).broadcast_to([P, JB, H // 2, HD]),
                                ALU.mult).then_inc(dve_freed, 1)

            def attn_out(n):
                v.tensor_copy(attnT[:], unit(n + 1, "aT")).then_inc(dve_freed, 1)

            def stats(m):
                for blk in range(JB):
                    v.bn_stats(bn[:, blk, :], res[:, blk, :]).then_inc(bn_done, 1)
                dve.wait_ge(bn_done, JB * (m + 1))
                stand_alone(dve)
                for blk in range(JB):
                    v.bn_aggr(mean_var[:, blk, :], bn[:, blk, :]).then_inc(aggr_done, 1)

            def residual(n):
                o = unit(n + 1, "y").rearrange("p (n c) -> p n c", n=JB)
                dve.wait_ge(xres_in, 16 * (n + 1))
                v.tensor_tensor(res[:], o, x_res[:], ALU.add).then_inc(dve_freed, 1)
                dve.wait_ge(dve_freed, ring.through(n + 1, "y"))
                stats(2 * n)

            def norm(n, which):
                dve.wait_ge(rstd_done, 2 * n + which + 1)
                dst = x1 if which == 0 else final
                for blk in range(JB):
                    v.tensor_scalar(dst[:, blk, :], res[:, blk, :], mean_var[:, blk, 0:1], rstd[:, blk:blk + 1],
                                    ALU.subtract, ALU.mult).then_inc(norm_done, 1)

            def x1_out(n):
                v.tensor_copy(x1T[:, 1:1 + T], unit(n + 1, "x1T")).then_inc(dve_freed, 1)

            def mix(n):
                dve.wait_ge(diff_done, n + 1)
                for dst, col, done in ((xk, 1, xk_done), (xr, 0, xr_done)):
                    v.scalar_tensor_tensor(out=dst[:], in0=x_diff[:], scalar=mu[:, col:col + 1],
                                           in1=x1T[:, 0:T], op0=ALU.mult, op1=ALU.add).then_inc(done, 1)

            def gate(n):
                o = unit(n + 1, "kv").rearrange("p (n c) -> p n c", n=JB)
                dve.wait_ge(act_freed, ring.through(n + 1, "rr"))
                v.scalar_tensor_tensor(out=gated[:].rearrange("p (n c) -> p n c", n=JB), in0=r_tanh[:], scalar=1.0, in1=o, op0=ALU.add,
                                       op1=ALU.mult).then_inc(dve_freed, 1)
                dve.wait_ge(dve_freed, ring.through(n + 1, "kv"))
                v.scalar_tensor_tensor(out=res[:], in0=gated[:].rearrange("p (n c) -> p n c", n=JB), scalar=0.5, in1=x1[:], op0=ALU.mult,
                                       op1=ALU.add).then_inc(gate_done, 1)
                dve.wait_ge(gate_done, n + 1)
                stats(2 * n + 1)

            PREP = {4: [(hi, Q)], 5: [(hi, K)], 6: [(features,), (mid, Q)], 7: [(hi, G), (mid, K), (hi, J)],
                    9: [(mid, G), (mid, J)]}
            POST = {4: [(sums_out,)], 5: [(normalise, 0), (normalise, 1)], 7: [(attn_out,)], 8: [(residual,)],
                    10: [(norm, 0)], 11: [(x1_out,)], 13: [(mix,)], 16: [(gate,)], 18: [(norm, 1)]}

            def period(b, par, post, prep):
                for t in range(PAIRS):
                    main(b, t)
                    if prep and t == 5:
                        values_in(b + 1, 1 - par)
                    for stage, *a in PREP.get(t, []) if prep else []:
                        stage(b + 1, *a)
                    for stage, *a in POST.get(t, []) if post else []:
                        stage(b - 1, *a)

            for t in sorted(PREP):
                if t == 5:
                    values_in(0, 0)
                for stage, *a in PREP[t]:
                    stage(0, *a)
            period(0, 0, False, True)
            with dve.Fori(1, B - 2, 2) as i:
                period(i, 1, True, True)
                period(i + 1, 0, True, True)
            period(B - 1, 1, True, False)
            for t in sorted(POST):
                for stage, *a in POST[t]:
                    stage(B - 1, *a)


INPUTS = ["L0_attn_x", "L0_attn_qkv_w", "L0_attn_out_w", "L0_attn_hex_w", "L0_attn_hamming_lambda_logit",
          "L0_attn_q6_w", "L0_attn_transforms", "L0_attn_transform_weights", "L0_attn_scale_logit",
          "L0_attn_sips_alpha", "L0_attn_sips_beta", "L0_ffn_W_r", "L0_ffn_W_k", "L0_ffn_W_v", "L0_ffn_mu_r",
          "L0_ffn_mu_k"]


def kernel(**inputs):
    import numpy as np
    import concourse.bacc as bacc
    from concourse import mybir as types
    from concourse.bass_utils import run_bass_kernel_spmd

    nc = bacc.Bacc("TRN2", target_bir_lowering=False, num_devices=1)
    arrays, args = {}, []
    for name in INPUTS:
        a = np.ascontiguousarray(inputs[name])
        a = a.reshape(a.shape or (1,))
        arrays[f"in_{name}"] = a
        args.append(nc.dram_tensor(f"in_{name}", a.shape, types.dt.from_np(a.dtype), kind="ExternalInput").ap())
    shape = inputs["L0_attn_x"].shape
    out = nc.dram_tensor("out", shape, types.dt.float32, kind="ExternalOutput").ap()
    build(nc, *args, out)
    return run_bass_kernel_spmd(nc, [arrays], core_ids=[0]).results[0]["out"]
```

```python
from contextlib import ExitStack

import concourse.bass as bass
from concourse import mybir
from concourse.alu_op_type import AluOpType as ALU

ACT = mybir.ActivationFunctionType
AX = mybir.AxisListType
F32 = mybir.dt.float32
BF16 = mybir.dt.bfloat16

DVE0_ONES = 1
DVE0_BETA = 7
DVE0_WEIGHTS = 11
DVE0_TWMAX = 13
DVE0_TW = 19
DVE0_TWT = 20
DVE0_LATTICE = 21
DVE0_ABS = 22
DVE0_SHIFT = 31
DVE0_END = 38

P = 128
LEVELS = 3
LN_EPS = 1e-5
TEMP = 0.5

QUADS = 4
PAIRS_PER_QUAD = 5
PAIRS = QUADS * PAIRS_PER_QUAD
LAST_OF_GROUP = [1, 1, 3, 3, 4]
PAIR_BUFFERS = 10
PSUM_PAIRS = 3
BIAS_LAG = 1
EXP_LAG = 2
VALUES_LAG = 6
Q, K, J, G = range(4)

PREP_UNITS = {0: ["xT"], 2: ["q"], 3: ["k"], 4: ["F"], 7: ["G"], 9: ["v"]}
POST_UNITS = {1: ["oT0"], 6: ["oT1"], 8: ["aT"], 10: ["y"], 14: ["x1T"], 16: ["kk"], 17: ["rr"], 18: ["kv"]}
ACT_UNITS = {"xT", "q", "k", "F", "kk", "rr"}


def period_uses(post, prep):
    uses = []
    for t in range(PAIRS):
        uses += PREP_UNITS.get(t, []) if prep else []
        uses += POST_UNITS.get(t, []) if post else []
    return uses


class Side:

    def __init__(self, batches):
        self.last = batches - 1
        self.prologue = self.first = period_uses(False, True)
        self.steady = period_uses(True, True)
        self.end = self.epilogue = period_uses(True, False)

    def uses(self, b):
        if not isinstance(b, int):
            return self.steady
        return {-1: self.prologue, 0: self.first, self.last: self.end,
                self.last + 1: self.epilogue}.get(b, self.steady)

    @staticmethod
    def of(uses, act):
        return sum((u in ACT_UNITS) == act for u in uses)

    def start(self, b, act):
        if isinstance(b, int) and b < 1:
            return 0 if b < 0 else self.of(self.prologue, act)
        if isinstance(b, int) and b > self.last:
            return self.start(self.last, act) + self.of(self.end, act)
        return (b - 1) * self.of(self.steady, act) + self.of(self.prologue + self.first, act)

    def through(self, b, use):
        act = use in ACT_UNITS
        uses = self.uses(b)
        return self.start(b, act) + self.of(uses[:uses.index(use) + 1], act)

    def before(self, b, use):
        n = self.uses(b).index(use)
        if n:
            last = self.uses(b)[n - 1]
            return last in ACT_UNITS, self.through(b, last)
        if isinstance(b, int) and b < 0:
            return None
        last = (self.uses(b - 1) if isinstance(b, int) else self.steady)[-1]
        assert last not in ACT_UNITS
        return False, self.start(b, False)


def build(nc, x, qkv_w, out_w, hex_w, lam_logit, q6_w, transforms, transform_weights, scale_logit,
          alpha, beta, w_r, w_k, w_v, mu_r, mu_k, out):
    B, T, D = x.shape
    H, NT = transform_weights.shape
    NB = hex_w.shape[0]
    HD = D // H
    JB = T // P
    assert D == P and H == 4 * QUADS and JB == 4 and B % 2 == 0
    QK_ROWS = LEVELS * LEVELS * HD
    LAT_ROWS = LEVELS * LEVELS * NB
    SHIFT_ROW = 2 * LAT_ROWS
    BIAS_ROWS = SHIFT_ROW + LEVELS
    HEX_J, HEX_I = 32, 96
    NP = HD * 2

    side_units = Side(B)

    with ExitStack() as ctx:
        def sb(name, shape, dt=F32):
            return ctx.enter_context(nc.sbuf_tensor(name, shape, dt))

        def sem(name):
            return ctx.enter_context(nc.semaphore(name))

        raw = ctx.enter_context(nc.psum_tensor("raw", [P, PSUM_PAIRS, 1024], F32))
        side_bank = ctx.enter_context(nc.psum_tensor("side_bank", [P, 512], F32))
        sums = ctx.enter_context(nc.psum_tensor("sums", [P, 512], F32))

        ident = sb("ident", [P, P])
        wqT = sb("wqT", [P, P])
        wkT = sb("wkT", [P, P])
        wvT = sb("wvT", [P, P])
        woT = sb("woT", [P, P])
        w_r_mix = [sb(f"w_r_mix{n}", [P, P]) for n in range(2)]
        w_k_mix = [sb(f"w_k_mix{n}", [P, P]) for n in range(2)]
        w_vT = sb("w_vT", [P, P])
        w_fT = sb("w_fT", [P, P])
        lat_map = sb("lat_map", [P, P])
        scal = sb("scal", [P, 4])
        tanhs = sb("tanhs", [P, 2])
        cols = sb("cols", [P, 8])
        mu = sb("mu", [P, 2])
        mu_prev = sb("mu_prev", [P, 2])
        tr_sb = sb("tr_sb", [NT, NB * NB])
        tw = sb("tw", [H, NT])
        tw_max = sb("tw_max", [H, 1])
        tw_exp = sb("tw_exp", [H, NT])
        tw_sum = sb("tw_sum", [H, 1])
        tw_inv = sb("tw_inv", [H, 1])
        twT = sb("twT", [NT, H])
        lat_abs = sb("lat_abs", [NB, H])
        shift_col = sb("shift_col", [P, LEVELS, 1], BF16)
        shift_f = sb("shift_f", [P, 2])
        j_scale = sb("j_scale", [P, 1])
        minus_half = sb("minus_half", [P, JB])

        q_stack = [sb(f"q_stack{n}", [QK_ROWS, H * T], BF16) for n in range(2)]
        k_stack = [sb(f"k_stack{n}", [QK_ROWS, H * T], BF16) for n in range(2)]
        i_stack = [sb(f"i_stack{n}", [BIAS_ROWS, H * T], BF16) for n in range(2)]
        j_stack = [sb(f"j_stack{n}", [BIAS_ROWS, T], BF16) for n in range(2)]
        values = [sb(f"values{n}", [P, JB, H, 32]) for n in range(2)]
        probs = sb("probs", [P, PAIR_BUFFERS, 2, T])
        w_nat = probs[:, 9].rearrange("p u (n c) -> p (u n) c", c=P)
        wo_perm = probs[:, 8, 0, 0:P]
        ones = probs[:, 8, 1, :]
        ones_rows = probs[0:H, 7].rearrange("p u i -> p (u i)").bitcast(BF16)[:, 0:LEVELS * T]
        shift_row = probs[0:1, 6].rearrange("p u i -> p (u i)").bitcast(BF16)[:, 0:LEVELS * T] \
            .rearrange("p (l i) -> p l i", l=LEVELS)

        x_nat = sb("x_nat", [P, JB, D])
        xT = sb("xT", [P, T])
        feats = sb("feats", [P, T])
        whole = sb("whole", [P, 4, T])
        parts = sb("parts", [P, 4, LEVELS, T], BF16)

        x_res = sb("x_res", [P, JB, D])
        sums_sb = sb("sums_sb", [P, 2, T])
        den_inv = sb("den_inv", [P, 2, JB, H // 2])
        attnT = sb("attnT", [P, T])
        res = sb("res", [P, JB, D])
        bn = sb("bn", [P, JB, 6])
        mean_var = sb("mean_var", [P, JB, 2])
        var_eps = sb("var_eps", [P, JB])
        rstd = sb("rstd", [P, JB])
        x1 = sb("x1", [P, JB, D])
        attn = x1
        x1T = sb("x1T", [P, 1 + T])
        gated = sb("gated", [P, JB, D])
        k_act = sb("k_act", [P, T])
        r_tanh = sb("r_tanh", [P, JB, D])
        final = sb("final", [P, JB, D])

        scratch = nc.dram_tensor("scratch", [3, LEVELS, P, T], BF16, kind="Internal").ap()
        lattice_i = nc.dram_tensor("lattice_i", [LEVELS, NB * H, T], BF16, kind="Internal").ap()
        hamming_i = nc.dram_tensor("hamming_i", [LEVELS, NB, T], BF16, kind="Internal").ap()
        ones_dram = nc.dram_tensor("ones_dram", [H, LEVELS * T], BF16, kind="Internal").ap()

        s_w, s_wf, s_w_late = sem("w_in"), sem("feature_w_in"), sem("late_w_in")
        s_beta, s_small, s_ident, s_zero = sem("beta_in"), sem("small_in"), sem("ident_made"), sem("zeroed")
        s_wT, s_wT_out = sem("w_transposed"), sem("w_copied")
        s_pool0 = sem("pool_setup")
        s_tanhs, s_twexp = sem("logit_tanhs"), sem("tw_exp_made")
        s_dve0 = sem("dve_setup")
        s_twT, s_lat, s_bound = sem("tw_transposed"), sem("lattice_product"), sem("bound_product")
        s_twT_out, s_lat_out, s_consts = sem("tw_copied"), sem("lattice_copied"), sem("consts_made")
        s_ones_d, s_const_rows = sem("ones_in_dram"), sem("const_rows_in")
        s_setup_psum = sem("setup_psum_read")

        raw_ready = sem("raw_ready")
        tanh_done = sem("tanh_done")
        bias_ready = sem("bias_ready")
        scores_done = sem("scores_done")
        exp_done = sem("exp_done")
        mask_done = sem("mask_done")
        pv_done = sem("pv_done")
        sums_read = sem("sums_read")

        dve_unit = sem("dve_unit")
        act_unit = sem("act_unit")
        dve_freed = sem("dve_freed")
        act_freed = sem("act_freed")

        x_in = sem("x_in")
        j_ready = sem("j_ready")
        hi_done, mid_done = sem("hi_done"), sem("mid_done")
        rest_done, lo_done = sem("rest_done"), sem("lo_done")
        SCR_DMAS = [1, 1, 1, 2]
        scr_in = [sem(f"scratch_in{n}") for n in range(4)]
        STACK_DMAS = [1, LEVELS, 2, 1 + LEVELS]
        stack_in = [sem(f"stack_in{n}") for n in range(4)]
        first_qk, first_g, second_in = sem("first_qk_in"), sem("first_g_in"), sem("second_in")

        xres_in = sem("xres_in")
        den_done, attn_done = sem("den_done"), sem("attn_done")
        res_done = sem("res_done")
        bn_done, aggr_done = sem("bn_done"), sem("aggr_done")
        eps_done, rstd_done = sem("eps_done"), sem("rstd_done")
        centred = sem("centred")
        norm_done = sem("norm_done")
        kact_done = sem("kact_done")
        gate_done = sem("gate_done")
        stored = sem("stored")

        passed = sem("passed")

        block = ctx.enter_context(nc.Block())

        def side_place(b, use):
            if isinstance(b, int) and b < 0 and use in ("q", "k"):
                u = "qk".index(use)
                return raw[:, 2, 512 * u:512 * (u + 1)]
            return side_bank[:]

        def pair_units(t):
            quad, p = divmod(t, PAIRS_PER_QUAD)
            if p < 2:
                return [[(4 * quad + r, 0, 0, T)] for r in (2 * p, 2 * p + 1)]
            if p < 4:
                return [[(4 * quad + r, 1, 0, 3 * P), (4 * quad + r, 3, 3 * P, P)] for r in (2 * p - 4, 2 * p - 3)]
            return [[(4 * quad + r, 2, (r % 2) * 2 * P, 2 * P) for r in (2 * u, 2 * u + 1)] for u in range(2)]

        def last_of_group(t):
            quad, p = divmod(t, PAIRS_PER_QUAD)
            return quad * PAIRS_PER_QUAD + LAST_OF_GROUP[p]

        def pair_probs(t):
            return probs[:, t % PAIR_BUFFERS]

        def lagged(b, t, lag):
            return (b, t - lag) if t >= lag else (b - 1, t - lag + PAIRS)

        def stand_alone(eng):
            eng.sem_inc(passed, 1)

        @block.sync
        def _(sp):
            sp.dma_start(x_nat[:], x[0].rearrange("(n p) c -> p n c", p=P)).then_inc(x_in, 16)
            sp.dma_start(w_nat[:, 0:3, :], qkv_w.rearrange("(t p) c -> p t c", p=P)).then_inc(s_w, 16)
            sp.wait_ge(s_zero, 1)
            for at, w in ((0, q6_w), (HEX_J, hex_w)):
                sp.dma_start(w_nat[at:at + LEVELS * NB, 7, :],
                             w.unsqueeze(0).broadcast_to([LEVELS, NB, D])).then_inc(s_wf, 16)
            sp.dma_start(w_nat[HEX_I:HEX_I + NB, 7, :], hex_w).then_inc(s_wf, 16)
            sp.dma_start(scal[:, 3:4], beta.partition_broadcast(P)).then_inc(s_beta, 16)
            for n, s in enumerate((lam_logit, scale_logit, alpha)):
                sp.dma_start(scal[:, n:n + 1], s.partition_broadcast(P)).then_inc(s_small, 16)
            sp.dma_start(tw[:], transform_weights).then_inc(s_small, 16)
            sp.dma_start(tr_sb[:], transforms.rearrange("t d e -> t (d e)")).then_inc(s_small, 16)
            sp.wait_ge(s_dve0, DVE0_ONES)
            sp.dma_start(ones_dram, ones_rows).then_inc(s_ones_d, 16)
            for n, w in enumerate((out_w, w_r, w_k, w_v)):
                sp.dma_start(w_nat[:, 3 + n, :], w).then_inc(s_w_late, 16)
            sp.dma_start(mu[:, 0:1], mu_r.rearrange("(p a) -> p a", a=1)).then_inc(s_w_late, 16)
            sp.dma_start(mu[:, 1:2], mu_k.rearrange("(p a) -> p a", a=1)).then_inc(s_w_late, 16)
            sp.wait_ge(s_ones_d, 16)
            for n in range(2):
                sp.dma_start(i_stack[n][SHIFT_ROW:BIAS_ROWS, :],
                             ones_dram.rearrange("h (l i) -> l h i", l=LEVELS)).then_inc(s_const_rows, 16)

            def to_dram(kind):
                done = scr_in[kind]
                if kind == G:
                    sp.dma_start(lattice_i.rearrange("l p i -> p l i"), parts[0:NB * H, G]).then_inc(done, 16)
                    sp.dma_start(hamming_i.rearrange("l p i -> p l i"),
                                 parts[HEX_I:HEX_I + NB, G]).then_inc(done, 16)
                else:
                    sp.dma_start(scratch[kind].rearrange("l p i -> p l i"), parts[:, kind]).then_inc(done, 16)

            def load_stack(kind, par, ready, heads=(0, H)):
                first, n = heads[0] * T, (heads[1] - heads[0]) * T
                if kind == Q:
                    src = scratch[Q].rearrange("l (d h) i -> (l d) (h i)", h=H)[:, first:first + n]
                    sp.dma_start(q_stack[par][:, first:first + n],
                                 src.unsqueeze(0).broadcast_to([LEVELS, LEVELS * HD, n])).then_inc(ready, 16)
                for level in range(LEVELS):
                    r, ham = level * LEVELS * HD, LAT_ROWS + level * LEVELS * NB
                    if kind == K:
                        src = scratch[K, level].rearrange("(d h) i -> d (h i)", h=H)[:, first:first + n]
                        sp.dma_start(k_stack[par][r:r + LEVELS * HD, first:first + n],
                                     src.unsqueeze(0).broadcast_to([LEVELS, HD, n])).then_inc(ready, 16)
                    if kind == G:
                        src = hamming_i.rearrange("l e i -> (l e) i").unsqueeze(1)
                        sp.dma_start(i_stack[par][ham:ham + LEVELS * NB, first:first + n].rearrange(
                                         "e (h i) -> e h i", i=T),
                                     src.broadcast_to([LEVELS * NB, n // T, T])).then_inc(ready, 16)
                if kind == J:
                    for at, row in ((0, 0), (LAT_ROWS, HEX_J)):
                        sp.dma_start(j_stack[par][at:at + LAT_ROWS, :],
                                     scratch[J][:, row:row + LEVELS * NB, :]).then_inc(ready, 16)
                if kind == G:
                    src = lattice_i.rearrange("l (e h) i -> (l e) (h i)", h=H)[:, first:first + n]
                    sp.dma_start(i_stack[par][0:LAT_ROWS, first:first + n],
                                 src.unsqueeze(0).broadcast_to([LEVELS, LEVELS * NB, n])).then_inc(ready, 16)

            def stacks(n, par):
                for kind in (Q, K, J, G):
                    sp.wait_ge(lo_done, 4 * n + kind + 1)
                    stand_alone(sp)
                    sp.wait_ge(stack_in[kind], 16 * STACK_DMAS[kind] * n)
                    to_dram(kind)
                if not (isinstance(n, int) and n < 2):
                    sp.wait_ge(raw_ready, PAIRS * (n - 1))
                    stand_alone(sp)
                    sp.wait_ge(bias_ready, PAIRS * (n - 1))
                for kind in (Q, K, J, G):
                    sp.wait_ge(scr_in[kind], 16 * SCR_DMAS[kind] * (n + 1))
                    load_stack(kind, par, stack_in[kind])

            def first_stacks():
                for kind in (Q, K):
                    sp.wait_ge(lo_done, kind + 1)
                    to_dram(kind)
                for kind in (Q, K):
                    sp.wait_ge(scr_in[kind], 16)
                    load_stack(kind, 0, first_qk, (0, 4))
                for kind in (J, G):
                    sp.wait_ge(lo_done, kind + 1)
                    to_dram(kind)
                sp.wait_ge(scr_in[J], 16)
                load_stack(J, 0, stack_in[J])
                sp.wait_ge(scr_in[G], 16 * SCR_DMAS[G])
                load_stack(G, 0, first_g, (0, 4))
                sp.wait_ge(s_consts, 1)
                for n in range(2):
                    sp.dma_start(j_stack[n][SHIFT_ROW:BIAS_ROWS, :], shift_row).then_inc(s_const_rows, 16)
                for kind in (Q, K, G):
                    load_stack(kind, 0, second_in, (4, 8))
                for kind in (Q, K, G):
                    load_stack(kind, 0, stack_in[kind], (8, H))

            def period(b, par, post, prep):
                if post:
                    sp.wait_ge(dve_freed, side_units.start(b, False))
                    stand_alone(sp)
                    sp.dma_start(x_res[:], x[b - 1].rearrange("(n p) c -> p n c", p=P)).then_inc(xres_in, 16)
                if prep:
                    stacks(b + 1, 1 - par)
                if post:
                    store(b - 1)

            def store(n):
                sp.wait_ge(norm_done, 2 * (n + 1))
                stand_alone(sp)
                sp.dma_start(out[n].rearrange("(n p) c -> p n c", p=P), final[:]).then_inc(stored, 16)
                sp.wait_ge(stored, 16 * (n + 1))
                stand_alone(sp)

            first_stacks()
            period(0, 0, False, True)
            with sp.Fori(1, B - 2, 2) as i:
                period(i, 1, True, True)
                period(i + 1, 0, True, True)
            period(B - 1, 1, True, False)
            sp.wait_ge(dve_freed, side_units.start(B - 1, False) + side_units.of(side_units.end, False))
            sp.dma_start(x_res[:], x[B - 1].rearrange("(n p) c -> p n c", p=P)).then_inc(xres_in, 16)
            store(B - 1)

        @block.tensor
        def _(pe):
            def mm(o, lhsT, rhs, start=True, stop=True, **kw):
                return nc.tensor.matmul(o, lhsT, rhs, start=start, stop=stop, **kw)

            def scores(b, par, t):
                first = isinstance(b, int) and b == 0
                if first and t == 0:
                    pe.wait_ge(first_qk, 16 * (1 + LEVELS))
                elif first and t == PAIRS_PER_QUAD:
                    pe.wait_ge(second_in, 16 * (1 + LEVELS + 1 + LEVELS))
                elif t == (2 * PAIRS_PER_QUAD if first else 0):
                    pe.wait_ge(stack_in[Q], 16 * STACK_DMAS[Q] * (b + 1))
                    pe.wait_ge(stack_in[K], 16 * STACK_DMAS[K] * (b + 1))
                if first and t < PSUM_PAIRS:
                    pe.wait_ge(s_dve0, DVE0_END if t else DVE0_WEIGHTS)
                else:
                    before = t - PSUM_PAIRS if t >= PSUM_PAIRS else \
                        max(o for o in range(PAIRS) if o % PSUM_PAIRS == t) - PAIRS
                    pe.wait_ge(scores_done, PAIRS * b + before + 1)
                for u, bank in enumerate(pair_units(t)):
                    for h, jb, at, n in bank:
                        last = mm(raw[:, t % PSUM_PAIRS, 512 * u + at:512 * u + at + n],
                                  k_stack[par][:, h * T + jb * P:h * T + (jb + 1) * P],
                                  q_stack[par][:, h * T + jb * P:(h + 1) * T])
                last.then_inc(raw_ready, 1)

            def biases(b, par, t):
                first = isinstance(b, int) and b == 0
                if t == 0:
                    pe.wait_ge(stack_in[J], 16 * STACK_DMAS[J] * (b + 1))
                if first and t == 0:
                    pe.wait_ge(first_g, 16 * (1 + LEVELS))
                    pe.wait_ge(s_const_rows, 16 * 4)
                elif t == (2 * PAIRS_PER_QUAD if first else 0):
                    pe.wait_ge(stack_in[G], 16 * STACK_DMAS[G] * (b + 1))
                pe.wait_ge(tanh_done, PAIRS * b + t + 1)
                for u, bank in enumerate(pair_units(t)):
                    for h, jb, at, n in bank:
                        last = mm(raw[:, t % PSUM_PAIRS, 512 * u + at:512 * u + at + n],
                                  j_stack[par][:, jb * P:(jb + 1) * P],
                                  i_stack[par][:, h * T + jb * P:(h + 1) * T])
                last.then_inc(bias_ready, 1)

            def weighted(b, par, t):
                quad, p = divmod(t, PAIRS_PER_QUAD)
                k, s = divmod(quad, 2)
                pe.wait_ge(mask_done, PAIRS * b + last_of_group(t) + 1)
                if t == 0:
                    pe.wait_ge(mid_done, 4 * (b + 1))
                if t == PAIRS // 2 or (t == 0 and not (isinstance(b, int) and b == 0)):
                    pe.wait_ge(sums_read, 2 * b + k)
                first_pair = last_of_group(t) - (1 if p < 4 else 0)

                def head(r, a, z):
                    return pair_probs(first_pair + (r // 2 if p < 4 else 0))[:, r % 2 if p < 4 else r // 2, a:z]

                jb, first, cols_of = [
                    (0, 0, lambda r: head(r, 0, T // 2)), (0, T // 2, lambda r: head(r, T // 2, T)),
                    (1, P, lambda r: head(r, 0, 3 * P)), (3, 3 * P, lambda r: head(r, 3 * P, T)),
                    (2, 2 * P, lambda r: head(r, (r % 2) * 2 * P, (r % 2 + 1) * 2 * P))][p]
                for r in range(4):
                    rhs = cols_of(r)
                    last = mm(sums[32 * r:32 * r + 32, first:first + rhs.shape[-1]],
                              values[par][:, jb, 4 * quad + r, :], rhs, start=(s == 0 and p == 0),
                              stop=(s == 1 and p == PAIRS_PER_QUAD - 1), skip_group_check=True)
                last.then_inc(pv_done, 1)

            def four(o, lhsT, rhs):
                for n in range(JB):
                    last = mm(o[:, n * P:(n + 1) * P], lhsT[:, n * P:(n + 1) * P], rhs)
                return last

            def four_transposes(o, src):
                for n in range(JB):
                    last = nc.tensor.transpose(o[:, n * P:(n + 1) * P], src(n), ident[:])
                return last

            def side(b, use):
                nx, pv = b + 1, b - 1
                o = side_place(b, use)
                before = side_units.before(b, use)
                if use == "F" and isinstance(b, int) and b < 0:
                    pe.wait_ge(act_freed, side_units.through(b, "xT"))
                elif before:
                    pe.wait_ge(act_freed if before[0] else dve_freed, before[1])
                done = act_unit if use in ACT_UNITS else dve_unit
                if use == "xT":
                    pe.wait_ge(x_in, 16 * (nx + 1))
                    last = four_transposes(o, lambda n: x_nat[:, n, :])
                elif use in ("q", "k"):
                    pe.wait_ge(act_freed, side_units.through(b, "xT"))
                    last = mm(o, wqT[:] if use == "q" else wkT[:], xT[:])
                elif use == "F":
                    last = mm(o, w_fT[:], xT[:])
                elif use == "v":
                    last = four(o, xT, wvT[:])
                elif use == "G":
                    pe.wait_ge(act_freed, side_units.through(b, "F"))
                    last = mm(o, lat_map[:], feats[:])
                elif use in ("oT0", "oT1"):
                    k = int(use[-1])
                    pe.wait_ge(sums_read, 2 * pv + 1 + k)
                    last = four_transposes(o, lambda n: sums_sb[:, k, n * P:(n + 1) * P])
                elif use == "aT":
                    pe.wait_ge(dve_freed, side_units.through(b, "oT1"))
                    last = four_transposes(o, lambda n: attn[:, n, :])
                elif use == "y":
                    pe.wait_ge(dve_freed, side_units.through(b, "aT"))
                    last = four(o, attnT, woT[:])
                elif use == "x1T":
                    pe.wait_ge(norm_done, 2 * pv + 1)
                    last = four_transposes(o, lambda n: x1[:, n, :])
                elif use == "kk":
                    pe.wait_ge(dve_freed, side_units.through(b, "x1T"))
                    mm(o, w_k_mix[0][:], x1T[:, 1:1 + T], stop=False)
                    last = mm(o, w_k_mix[1][:], x1T[:, 0:T], start=False)
                elif use == "rr":
                    pe.wait_ge(dve_freed, side_units.through(b, "x1T"))
                    for n in range(JB):
                        mm(o[:, n * P:(n + 1) * P], x1T[:, 1 + n * P:1 + (n + 1) * P], w_r_mix[0][:], stop=False)
                        last = mm(o[:, n * P:(n + 1) * P], x1T[:, n * P:(n + 1) * P], w_r_mix[1][:], start=False)
                elif use == "kv":
                    pe.wait_ge(kact_done, pv + 1)
                    last = four(o, k_act, w_vT[:])
                last.then_inc(done, 1)

            def period(b, par, post, prep):
                for t in range(PAIRS):
                    def ahead():
                        if t + 1 < PAIRS:
                            scores(b, par, t + 1)
                        elif prep:
                            scores(b + 1, 1 - par, 0)

                    def lag(stage, lag):
                        if t >= lag or post:
                            batch, pair = lagged(b, t, lag)
                            stage(batch, par if t >= lag else 1 - par, pair)

                    lag(biases, BIAS_LAG)
                    for use in (PREP_UNITS.get(t, []) if prep else []) + (POST_UNITS.get(t, []) if post else []):
                        side(b, use)
                    lag(weighted, VALUES_LAG)
                    ahead()

            def transposed(out, names):
                for n, src in enumerate(names):
                    last = nc.tensor.transpose(out[:, n * P:(n + 1) * P], src, ident[:])
                return last

            pe.wait_ge(s_ident, 1)
            side(-1, "xT")
            pe.wait_ge(s_w, 16)
            pe.wait_ge(s_wf, 16 * 3)
            transposed(raw[:, 0], [w_nat[:, n, :] for n in (0, 1, 7, 2)]).then_inc(s_wT, 1)
            pe.wait_ge(s_dve0, DVE0_WEIGHTS)
            for use in ("q", "k", "F"):
                side(-1, use)
            pe.wait_ge(s_dve0, DVE0_TW)
            nc.tensor.transpose(raw[0:NT, 1, 0:H], tw[:], ident[0:H, 0:H]).then_inc(s_twT, 1)
            pe.wait_ge(s_dve0, DVE0_TWT)
            for e in range(NB):
                last = mm(raw[0:NB, 1, 512 + e * H:512 + (e + 1) * H],
                          tr_sb[:].rearrange("t (d e) -> t d e", e=NB)[:, :, e], twT[:])
            last.then_inc(s_lat, 1)
            pe.wait_ge(s_dve0, DVE0_LATTICE)
            side(-1, "G")
            pe.wait_ge(s_dve0, DVE0_ABS)
            mm(raw[:, 1, 0:H], ones[0:NB, 0:P], lat_abs[:]).then_inc(s_bound, 1)
            side(-1, "v")
            scores(0, 0, 0)
            pe.wait_ge(s_w_late, 16 * 6)
            pe.wait_ge(s_zero, 2)
            transposed(raw[:, 2], [wo_perm] + [w_nat[:, n, :] for n in (4, 5, 6)]).then_inc(s_wT, 1)
            period(0, 0, False, True)
            with pe.Fori(1, B - 2, 2) as i:
                period(i, 1, True, True)
                period(i + 1, 0, True, True)
            period(B - 1, 1, True, False)
            for t in range(PAIRS - BIAS_LAG, PAIRS):
                biases(B - 1, 1, t)
            for t in range(PAIRS - VALUES_LAG, PAIRS):
                weighted(B - 1, 1, t)
            for t in sorted(POST_UNITS):
                for use in POST_UNITS[t]:
                    side(B, use)

        @block.scalar
        def _(act):
            def tanh(b, t):
                act.wait_ge(raw_ready, PAIRS * b + t + 1)
                if not (isinstance(b, int) and b == 0 and t < PAIR_BUFFERS):
                    act.wait_ge(pv_done, PAIRS * b + last_of_group(t) - PAIR_BUFFERS + 1)
                nc.scalar.activation(pair_probs(t), raw[:, t % PSUM_PAIRS, :].rearrange("p (u i) -> p u i", u=2),
                                     ACT.Tanh).then_inc(tanh_done, 1)

            def exp(b, t):
                act.wait_ge(scores_done, PAIRS * b + t + 1)
                nc.scalar.activation(pair_probs(t), pair_probs(t), ACT.Exp).then_inc(exp_done, 1)

            def side(b, use):
                nx, pv = b + 1, b - 1
                early = isinstance(b, int) and b < 0
                o = side_place(b, use)
                act.wait_ge(act_unit, side_units.through(b, use))
                if use == "xT":
                    ins = nc.scalar.activation(xT[:], o, ACT.Copy)
                elif use in ("q", "k"):
                    kind = Q if use == "q" else K
                    if early:
                        act.wait_ge(s_dve0, DVE0_BETA)
                    else:
                        act.wait_ge(lo_done, 4 * (nx - 1) + kind + 1)
                    ins = nc.scalar.activation(whole[:, kind, :], o, ACT.Copy,
                                               scale=cols[:, 2:3] if use == "q" else 1.0)
                elif use == "F":
                    if not early:
                        act.wait_ge(j_ready, nx)
                    ins = nc.scalar.activation(feats[:], o, ACT.Tanh)
                elif use == "kk":
                    ins = nc.scalar.activation(k_act[:], o, ACT.Relu)
                elif use == "rr":
                    ins = nc.scalar.activation(r_tanh[:].rearrange("p n c -> p (n c)"), o, ACT.Tanh, scale=0.5)
                ins.then_inc(act_freed, 1)
                if use == "kk":
                    act.wait_ge(act_freed, side_units.through(b, "kk"))
                    nc.scalar.activation(k_act[:], k_act[:], ACT.Square).then_inc(kact_done, 1)

            def sides(b, t, post, prep):
                for use in (PREP_UNITS.get(t, []) if prep else []) + (POST_UNITS.get(t, []) if post else []):
                    if use in ACT_UNITS:
                        side(b, use)

            def period(b, par, post, prep):
                if prep:
                    act.wait_ge(act_unit, side_units.start(b, True))
                    act.dma_start(x_nat[:], x[b + 1].rearrange("(n p) c -> p n c", p=P)).then_inc(x_in, 16)
                for t in range(PAIRS):
                    tanh(b, t)
                    if t >= EXP_LAG or post:
                        exp(*lagged(b, t, EXP_LAG))
                    sides(b, t, post, prep)

            side(-1, "xT")
            side(-1, "q")
            act.wait_ge(s_small, 16 * 5)
            nc.scalar.activation(tanhs[:], scal[:, 0:2], ACT.Tanh, scale=0.5).then_inc(s_tanhs, 1)
            act.wait_ge(s_dve0, DVE0_TWMAX)
            nc.scalar.activation(tw_exp[:], tw[:], ACT.Exp, bias=tw_max[:], scale=1.0 / TEMP,
                                 accum_out=tw_sum[:]).then_inc(s_twexp, 1)
            side(-1, "k")
            side(-1, "F")
            act.wait_ge(s_dve0, DVE0_SHIFT)
            nc.scalar.activation(shift_row, shift_col[0:1].broadcast_to([1, LEVELS, T]),
                                 ACT.Copy).then_inc(s_consts, 1)
            period(0, 0, False, True)
            with act.Fori(1, B - 2, 2) as i:
                period(i, 1, True, True)
                period(i + 1, 0, True, True)
            period(B - 1, 1, True, False)
            for t in range(PAIRS - EXP_LAG, PAIRS):
                exp(B - 1, t)
            for t in sorted(POST_UNITS):
                for use in POST_UNITS[t]:
                    if use in ACT_UNITS:
                        side(B, use)

        @block.gpsimd
        def _(pool):
            nc.gpsimd.memset(ident[:], 0.0).then_inc(s_pool0, 1)
            pool.wait_ge(s_pool0, 1)
            nc.gpsimd.affine_select(out=ident[:], in_=ident[:], compare_op=ALU.not_equal, fill=1.0, base=0,
                                    pattern=[[-1, P]], channel_multiplier=1).then_inc(s_ident, 1)
            for n in range(2):
                nc.gpsimd.memset(values[n][:], 0.0).then_inc(s_pool0, 1)
            pool.wait_ge(s_pool0, 3)
            for n in range(2):
                for s in range(2):
                    v = values[n][:].rearrange("p j (k s r) m -> p (j k) s r m", k=2, s=2)
                    nc.gpsimd.memset(v[:, :, s, :, NP * s + HD], 1.0).then_inc(s_pool0, 1)

            def mask(b, t):
                v, p = pair_probs(t), t % PAIRS_PER_QUAD
                if p < 4:
                    blocks = [v[:, :, 0:P]] + ([v[:, :, 3 * P:T]] if p >= 2 else [])
                else:
                    blocks = [v.rearrange("p u (r i) -> p (u r) i", r=2)[:, :, 0:P]]
                pool.wait_ge(exp_done, PAIRS * b + t + 1)
                stand_alone(pool)
                for v in blocks:
                    last = nc.gpsimd.affine_select(out=v, in_=v, compare_op=ALU.is_ge, fill=0.0, base=0,
                                                   pattern=[[0, v.shape[1]], [1, P]], channel_multiplier=-1)
                last.then_inc(mask_done, 1)

            def rest(n, kind):
                pool.wait_ge(hi_done, 4 * n + kind + 1)
                w = whole[:, kind, :]
                nc.gpsimd.tensor_tensor(w, w, parts[:, kind, 0, :], ALU.subtract).then_inc(rest_done, 1)

            def lo(n, kind):
                pool.wait_ge(mid_done, 4 * n + kind + 1)
                nc.gpsimd.tensor_tensor(parts[:, kind, 2, :], whole[:, kind, :], parts[:, kind, 1, :],
                                        ALU.subtract).then_inc(lo_done, 1)

            def inv_std(n, which):
                m = 2 * n + which
                pool.wait_ge(aggr_done, JB * (m + 1))
                stand_alone(pool)
                nc.gpsimd.tensor_scalar(var_eps[:], mean_var[:, :, 1], LN_EPS, None, ALU.add).then_inc(eps_done, 1)
                pool.wait_ge(eps_done, m + 1)
                nc.gpsimd.tensor_tensor(rstd[:], var_eps[:], minus_half[:], ALU.pow).then_inc(rstd_done, 1)

            def norm(n, which):
                dst, m = x1 if which == 0 else final, 2 * n + which
                nc.gpsimd.tensor_tensor(dst[:], res[:], mean_var[:, :, 0:1].broadcast_to([P, JB, D]),
                                        ALU.subtract).then_inc(centred, 1)
                pool.wait_ge(rstd_done, m + 1)
                pool.wait_ge(centred, m + 1)
                nc.gpsimd.tensor_tensor(dst[:], dst[:], rstd[:].unsqueeze(2).broadcast_to([P, JB, D]),
                                        ALU.mult).then_inc(norm_done, 1)

            PREP = {4: [(rest, Q)], 5: [(rest, K)], 6: [(rest, J)], 7: [(lo, Q)], 8: [(lo, K), (rest, G)], 9: [(lo, J)], 10: [(lo, G)]}
            POST = {11: [(inv_std, 0)], 12: [(norm, 0)], 19: [(inv_std, 1), (norm, 1)]}

            def period(b, par, post, prep):
                for t in range(PAIRS):
                    if t >= EXP_LAG or post:
                        mask(*lagged(b, t, EXP_LAG))
                    for stage, *a in PREP.get(t, []) if prep else []:
                        stage(b + 1, *a)
                    for stage, *a in POST.get(t, []) if post else []:
                        stage(b - 1, *a)

            for kind in (K, J):
                rest(0, kind)
                lo(0, kind)
            period(0, 0, False, True)
            with pool.Fori(1, B - 2, 2) as i:
                period(i, 1, True, True)
                period(i + 1, 0, True, True)
            period(B - 1, 1, True, False)
            for t in range(PAIRS - EXP_LAG, PAIRS):
                mask(B - 1, t)
            for t in sorted(POST):
                for stage, *a in POST[t]:
                    stage(B - 1, *a)

        @block.vector
        def _(dve):
            made = [0]

            def link(ins):
                made[0] += 1
                ins.then_inc(s_dve0, 1)
                dve.wait_ge(s_dve0, made[0])

            def mark(value):
                assert made[0] == value, (made[0], value)

            v = nc.vector

            def main(b, t):
                dve.wait_ge(bias_ready, PAIRS * b + t + 1)
                dve.wait_ge(tanh_done, PAIRS * b + t + 1)
                o = pair_probs(t)
                v.scalar_tensor_tensor(out=o, in0=o, scalar=scal[:, 2:3],
                                       in1=raw[:, t % PSUM_PAIRS, :].rearrange("p (u i) -> p u i", u=2),
                                       op0=ALU.mult, op1=ALU.add).then_inc(scores_done, 1)

            def unit(b, use):
                dve.wait_ge(dve_unit, side_units.through(b, use))
                return side_bank[:]

            def hi(n, kind):
                if kind in (Q, K):
                    dve.wait_ge(act_freed, side_units.through(n - 1, "qk"[kind]))
                elif kind == G:
                    dve.wait_ge(dve_freed, side_units.through(n - 1, "G"))
                else:
                    dve.wait_ge(j_ready, n + 1)
                if not (isinstance(n, int) and n == 0):
                    dve.wait_ge(scr_in[kind], 16 * SCR_DMAS[kind] * n)
                v.tensor_copy(parts[:, kind, 0, :], whole[:, kind, :]).then_inc(hi_done, 1)

            def mid(n, kind):
                dve.wait_ge(rest_done, 4 * n + kind + 1)
                v.tensor_copy(parts[:, kind, 1, :], whole[:, kind, :]).then_inc(mid_done, 1)

            def values_in(n):
                o = unit(n - 1, "v")
                if isinstance(n, int) and n < 2:
                    dve.wait_ge(s_pool0, 3 + 4)
                else:
                    dve.wait_ge(pv_done, PAIRS * (n - 1))
                for s in range(2):
                    dst = values[parity[0]][:].rearrange("p j (k s r) m -> p (j k) s r m", k=2, s=2)
                    src = o.rearrange("p (j s r d) -> p j s r d", s=2, r=4, d=HD)
                    last = v.tensor_copy(dst[:, :, s, :, NP * s:NP * s + HD], src[:, :, s])
                last.then_inc(dve_freed, 1)

            def features_j(n):
                dve.wait_ge(act_freed, side_units.through(n - 1, "F"))
                if not (isinstance(n, int) and n == 0):
                    dve.wait_ge(lo_done, 4 * n)
                v.tensor_scalar(whole[:, J, :], feats[:], j_scale[:], None, ALU.mult).then_inc(j_ready, 1)

            def features_i(n):
                v.tensor_copy(whole[:, G, :], unit(n - 1, "G")).then_inc(dve_freed, 1)

            def sums_out(n, k):
                dve.wait_ge(pv_done, PAIRS * n + (k + 1) * PAIRS // 2)
                v.tensor_copy(sums_sb[:, k, :], sums[:]).then_inc(sums_read, 1)

            def normalise(n, k):
                o = unit(n + 1, f"oT{k}").rearrange("p (n q m) -> p n q m", n=JB, m=NP)
                v.reciprocal(den_inv[:, k], o[:, :, :, HD]).then_inc(den_done, 1)
                dve.wait_ge(den_done, 2 * n + k + 1)
                dst = attn[:].rearrange("p n (k q d) -> p n k q d", k=2, d=HD)[:, :, k]
                v.tensor_tensor(dst, o[:, :, :, 0:HD],
                                den_inv[:, k].unsqueeze(3).broadcast_to([P, JB, H // 2, HD]),
                                ALU.mult).then_inc(dve_freed, 1)

            def attn_out(n):
                v.tensor_copy(attnT[:], unit(n + 1, "aT")).then_inc(dve_freed, 1)

            def stats(n, which):
                if which == 0:
                    dve.wait_ge(dve_freed, side_units.through(n + 1, "y"))
                else:
                    dve.wait_ge(gate_done, n + 1)
                for blk in range(JB):
                    v.bn_stats(bn[:, blk, :], res[:, blk, :]).then_inc(bn_done, 1)
                dve.wait_ge(bn_done, JB * (2 * n + which + 1))
                stand_alone(dve)
                for blk in range(JB):
                    v.bn_aggr(mean_var[:, blk, :], bn[:, blk, :]).then_inc(aggr_done, 1)

            def residual(n):
                o = unit(n + 1, "y").rearrange("p (n c) -> p n c", n=JB)
                dve.wait_ge(xres_in, 16 * (n + 1))
                v.tensor_tensor(res[:], o, x_res[:], ALU.add).then_inc(dve_freed, 1)

            def x1_out(n):
                v.tensor_copy(x1T[:, 1:1 + T], unit(n + 1, "x1T")).then_inc(dve_freed, 1)

            def gate(n):
                o = unit(n + 1, "kv").rearrange("p (n c) -> p n c", n=JB)
                dve.wait_ge(act_freed, side_units.through(n + 1, "rr"))
                v.scalar_tensor_tensor(out=gated[:], in0=r_tanh[:], scalar=1.0, in1=o, op0=ALU.add,
                                       op1=ALU.mult).then_inc(dve_freed, 1)
                dve.wait_ge(dve_freed, side_units.through(n + 1, "kv"))
                v.scalar_tensor_tensor(out=res[:], in0=gated[:], scalar=0.5, in1=x1[:], op0=ALU.mult,
                                       op1=ALU.add).then_inc(gate_done, 1)

            PREP = {2: [(hi, Q)], 3: [(hi, K)], 4: [(features_j,)], 5: [(hi, J)], 6: [(mid, Q)], 7: [(features_i,), (hi, G), (mid, K)], 8: [(mid, J)], 9: [(values_in,), (mid, G)]}
            POST = {1: [(normalise, 0)], 6: [(normalise, 1)], 8: [(attn_out,)], 10: [(residual,), (stats, 0)], 14: [(x1_out,)], 18: [(gate,)], 19: [(stats, 1)]}

            def period(b, par, post, prep):
                parity[0] = 1 - par
                for t in range(PAIRS):
                    if t == 5 and post:
                        sums_out(b - 1, 1)
                    if t == 5 + PAIRS // 2:
                        sums_out(b, 0)
                    if t >= BIAS_LAG or post:
                        main(*lagged(b, t, BIAS_LAG))
                    for stage, *a in PREP.get(t, []) if prep else []:
                        stage(b + 1, *a)
                    for stage, *a in POST.get(t, []) if post else []:
                        stage(b - 1, *a)

            def rest_here(kind):
                dve.wait_ge(hi_done, kind + 1)
                dve.wait_ge(rest_done, kind) if kind else None
                w = whole[:, kind, :]
                v.tensor_tensor(w, w, parts[:, kind, 0, :], ALU.subtract).then_inc(rest_done, 1)

            def lo_here(kind):
                dve.wait_ge(mid_done, kind + 1)
                dve.wait_ge(lo_done, kind) if kind else None
                v.tensor_tensor(parts[:, kind, 2, :], whole[:, kind, :], parts[:, kind, 1, :],
                                ALU.subtract).then_inc(lo_done, 1)

            parity = [0]
            v.memset(w_nat[:, 7, :], 0.0).then_inc(s_zero, 1)
            link(v.memset(ones_rows, 1.0))
            mark(DVE0_ONES)
            link(v.memset(minus_half[:], -0.5))
            link(v.memset(x1T[:, 0:1], 0.0))
            link(v.memset(lat_map[:], 0.0))
            link(v.memset(j_scale[:], 1.0))
            link(v.memset(ones, 1.0))
            dve.wait_ge(s_beta, 16)
            link(v.reciprocal(cols[:, 2:3], scal[:, 3:4]))
            mark(DVE0_BETA)
            dve.wait_ge(s_wT, 1)
            for n, w in enumerate((wqT, wkT)):
                link(v.tensor_copy(w[:].rearrange("p (d h) -> p d h", h=H),
                                   raw[:, 0, n * P:(n + 1) * P].rearrange("p (h d) -> p d h", h=H)))
            link(v.tensor_copy(w_fT[:], raw[:, 0, 2 * P:3 * P]))
            link(v.tensor_copy(wvT[:], raw[:, 0, 3 * P:4 * P]))
            mark(DVE0_WEIGHTS)
            dve.wait_ge(s_small, 16 * 5)
            link(v.tensor_reduce(tw_sum[:], tw[:], AX.X, ALU.max))
            link(v.tensor_scalar(tw_max[:], tw_sum[:], -1.0 / TEMP, None, ALU.mult))
            mark(DVE0_TWMAX)
            hi(0, Q)
            rest_here(Q)
            mid(0, Q)
            hi(0, K)
            lo_here(Q)
            dve.wait_ge(s_tanhs, 1)
            link(v.tensor_scalar(cols[:, 0:1], tanhs[:, 0:1], 0.25, 0.25, ALU.mult, ALU.add))
            link(v.tensor_scalar(cols[:, 1:2], tanhs[:, 1:2], 1.0 / NB, 1.0 / NB, ALU.mult, ALU.add))
            link(v.tensor_copy(j_scale[HEX_J:HEX_J + LEVELS * NB, :], cols[HEX_J:HEX_J + LEVELS * NB, 0:1]))
            dve.wait_ge(s_ident, 1)
            link(v.tensor_copy(lat_map[HEX_I:P, HEX_I:P], ident[HEX_I:P, HEX_I:P]))
            dve.wait_ge(s_twexp, 1)
            link(v.reciprocal(tw_inv[:], tw_sum[:]))
            link(v.tensor_scalar(tw[:], tw_exp[:], tw_inv[:], None, ALU.mult))
            mark(DVE0_TW)
            mid(0, K)
            dve.wait_ge(s_twT, 1)
            link(v.tensor_copy(twT[:], raw[0:NT, 1, 0:H]))
            mark(DVE0_TWT)
            features_j(0)
            hi(0, J)
            dve.wait_ge(s_lat, 1)
            link(v.tensor_scalar(lat_map[0:NB, 0:NB * H], raw[0:NB, 1, 512:512 + NB * H], cols[0:NB, 1:2], None,
                                 ALU.mult))
            mark(DVE0_LATTICE)
            link(v.tensor_reduce(lat_abs[:], lat_map[0:NB, 0:NB * H].rearrange("d (e h) -> d h e", h=H), AX.X,
                                 ALU.add, apply_absolute_value=True))
            mark(DVE0_ABS)
            link(v.scalar_tensor_tensor(out=cols[:, 3:4], in0=scal[:, 2:3], scalar=-1.0, in1=scal[:, 2:3],
                                        op0=ALU.mult, op1=ALU.max))
            link(v.scalar_tensor_tensor(out=cols[:, 4:5], in0=cols[:, 0:1], scalar=float(NB), in1=cols[:, 3:4],
                                        op0=ALU.mult, op1=ALU.add))
            features_i(0)
            hi(0, G)
            mid(0, J)
            rest_here(G)
            mid(0, G)
            lo_here(G)
            dve.wait_ge(s_bound, 1)
            link(v.tensor_reduce(cols[:, 5:6], raw[:, 1, 0:H], AX.X, ALU.max))
            link(v.scalar_tensor_tensor(out=cols[:, 6:7], in0=cols[:, 4:5], scalar=-1.0, in1=cols[:, 5:6],
                                        op0=ALU.mult, op1=ALU.subtract))
            link(v.tensor_copy(shift_col[:, 0], cols[:, 6:7]))
            link(v.tensor_tensor(shift_f[:, 0:1], cols[:, 6:7], shift_col[:, 0], ALU.subtract))
            link(v.tensor_copy(shift_col[:, 1], shift_f[:, 0:1]))
            link(v.tensor_tensor(shift_f[:, 1:2], shift_f[:, 0:1], shift_col[:, 1], ALU.subtract))
            link(v.tensor_copy(shift_col[:, 2], shift_f[:, 1:2]))
            mark(DVE0_SHIFT)
            values_in(0)
            dve.wait_ge(s_w_late, 16 * 6)
            for k in range(2):
                for s in range(2):
                    src = w_nat[:, 3, :].rearrange("p (k s r d) -> p k s r d", k=2, s=2, r=4)[:, k, s]
                    dst = wo_perm.rearrange("p (k r s d) -> p k r s d", k=2, s=2, r=4)[:, k, :, s]
                    last = v.tensor_copy(dst, src)
            last.then_inc(s_zero, 1)
            link(v.tensor_scalar(mu_prev[:], mu[:], -1.0, 1.0, ALU.mult, ALU.add))
            dve.wait_ge(s_wT, 2)
            link(v.tensor_copy(woT[:], raw[:, 2, 0:P]))
            for n, w in enumerate((w_r_mix, w_k_mix)):
                src = raw[:, 2, (n + 1) * P:(n + 2) * P]
                link(v.tensor_scalar(w[0][:], src, mu[:, n:n + 1], None, ALU.mult))
                link(v.tensor_scalar(w[1][:], src, mu_prev[:, n:n + 1], None, ALU.mult))
            link(v.tensor_copy(w_vT[:], raw[:, 2, 3 * P:4 * P]))
            mark(DVE0_END)

            period(0, 0, False, True)
            with dve.Fori(1, B - 2, 2) as i:
                period(i, 1, True, True)
                period(i + 1, 0, True, True)
            period(B - 1, 1, True, False)
            for t in range(PAIRS - BIAS_LAG, PAIRS):
                main(B - 1, t)
            sums_out(B - 1, 1)
            for t in sorted(POST):
                for stage, *a in POST[t]:
                    stage(B - 1, *a)


INPUTS = ["L0_attn_x", "L0_attn_qkv_w", "L0_attn_out_w", "L0_attn_hex_w", "L0_attn_hamming_lambda_logit",
          "L0_attn_q6_w", "L0_attn_transforms", "L0_attn_transform_weights", "L0_attn_scale_logit",
          "L0_attn_sips_alpha", "L0_attn_sips_beta", "L0_ffn_W_r", "L0_ffn_W_k", "L0_ffn_W_v", "L0_ffn_mu_r",
          "L0_ffn_mu_k"]


def kernel(**inputs):
    import numpy as np
    import concourse.bacc as bacc
    from concourse import mybir as types
    from concourse.bass_utils import run_bass_kernel_spmd

    nc = bacc.Bacc("TRN2", target_bir_lowering=False, num_devices=1,
                   dynamic_dma_scratch_size=8192)
    arrays, args = {}, []
    for name in INPUTS:
        a = np.ascontiguousarray(inputs[name])
        a = a.reshape(a.shape or (1,))
        arrays[f"in_{name}"] = a
        args.append(nc.dram_tensor(f"in_{name}", a.shape, types.dt.from_np(a.dtype), kind="ExternalInput").ap())
    shape = inputs["L0_attn_x"].shape
    out = nc.dram_tensor("out", shape, types.dt.float32, kind="ExternalOutput").ap()
    build(nc, *args, out)
    return run_bass_kernel_spmd(nc, [arrays], core_ids=[0]).results[0]["out"]
```

```python
from contextlib import ExitStack

import concourse.bass as bass
from concourse import mybir
from concourse.alu_op_type import AluOpType as ALU

ACT = mybir.ActivationFunctionType
AX = mybir.AxisListType
F32 = mybir.dt.float32
BF16 = mybir.dt.bfloat16

DVE0_ONES = 1
DVE0_BETA = 6
DVE0_WEIGHTS = 10
DVE0_TWMAX = 12
DVE0_TW = 17
DVE0_TWT = 18
DVE0_LATTICE = 19
DVE0_ABS = 20
DVE0_SHIFT = 30
DVE0_END = 37

P = 128
LEVELS = 3
LN_EPS = 1e-5
SAFE_SCORE = 75.0
TEMP = 0.5

QUADS = 4
PAIRS_PER_QUAD = 5
PAIRS = QUADS * PAIRS_PER_QUAD
LAST_OF_GROUP = [1, 1, 3, 3, 4]
PAIR_BUFFERS = 10
PSUM_PAIRS = 3
BIAS_LAG = 1
EXP_LAG = 3
VALUES_STEPS = [6, 7, 7, 9, 11, 11, 12, 13, 14, 15, 16, 18, 19, 19, 19, 20, 20, 24, 25, 25]
Q, K, J, G = range(4)

PREP_UNITS = {0: ["xT"], 2: ["q"], 3: ["k"], 5: ["F"], 7: ["G"], 9: ["v"]}
POST_UNITS = {1: ["oT0"], 6: ["oT1"], 8: ["aT"], 10: ["y"], 14: ["x1T"], 16: ["kk"], 17: ["rr"], 18: ["kv"]}
AHEAD_FIRST = [2, 3, 4, 7, 9, 18]
ACT_UNITS = {"F", "kk", "rr"}


def period_uses(post, prep):
    uses = []
    for t in range(PAIRS):
        uses += PREP_UNITS.get(t, []) if prep else []
        uses += POST_UNITS.get(t, []) if post else []
    return uses


class Side:

    def __init__(self, batches):
        self.last = batches - 1
        self.prologue = self.first = period_uses(False, True)
        self.steady = period_uses(True, True)
        self.end = self.epilogue = period_uses(True, False)

    def uses(self, b):
        if not isinstance(b, int):
            return self.steady
        return {-1: self.prologue, 0: self.first, self.last: self.end,
                self.last + 1: self.epilogue}.get(b, self.steady)

    @staticmethod
    def of(uses, act):
        return sum((u in ACT_UNITS) == act for u in uses)

    def start(self, b, act):
        if isinstance(b, int) and b < 1:
            return 0 if b < 0 else self.of(self.prologue, act)
        if isinstance(b, int) and b > self.last:
            return self.start(self.last, act) + self.of(self.end, act)
        return (b - 1) * self.of(self.steady, act) + self.of(self.prologue + self.first, act)

    def through(self, b, use):
        act = use in ACT_UNITS
        uses = self.uses(b)
        return self.start(b, act) + self.of(uses[:uses.index(use) + 1], act)

    def before(self, b, use):
        n = self.uses(b).index(use)
        if n:
            last = self.uses(b)[n - 1]
            return last in ACT_UNITS, self.through(b, last)
        if isinstance(b, int) and b < 0:
            return None
        last = (self.uses(b - 1) if isinstance(b, int) else self.steady)[-1]
        assert last not in ACT_UNITS
        return False, self.start(b, False)


def build(nc, x, qkv_w, out_w, hex_w, lam_logit, q6_w, transforms, transform_weights, scale_logit,
          alpha, beta, w_r, w_k, w_v, mu_r, mu_k, out):
    B, T, D = x.shape
    H, NT = transform_weights.shape
    NB = hex_w.shape[0]
    HD = D // H
    JB = T // P
    assert D == P and H == 4 * QUADS and JB == 4 and B % 2 == 0
    QK_ROWS = LEVELS * LEVELS * HD
    LAT_ROWS = LEVELS * LEVELS * NB
    SHIFT_ROW = 2 * LAT_ROWS
    BIAS_ROWS = SHIFT_ROW + LEVELS
    HEX_J, HEX_I = 32, 96
    NP = HD * 2

    side_units = Side(B)

    with ExitStack() as ctx:
        def sb(name, shape, dt=F32):
            return ctx.enter_context(nc.sbuf_tensor(name, shape, dt))

        def sem(name):
            return ctx.enter_context(nc.semaphore(name))

        raw = ctx.enter_context(nc.psum_tensor("raw", [P, PSUM_PAIRS, 1024], F32))
        side_bank = ctx.enter_context(nc.psum_tensor("side_bank", [P, 512], F32))
        sums = ctx.enter_context(nc.psum_tensor("sums", [P, 512], F32))

        ident = sb("ident", [P, P])
        wqT = sb("wqT", [P, P])
        wkT = sb("wkT", [P, P])
        wvT = sb("wvT", [P, P])
        woT = sb("woT", [P, P])
        w_r_mix = [sb(f"w_r_mix{n}", [P, P]) for n in range(2)]
        w_k_mix = [sb(f"w_k_mix{n}", [P, P]) for n in range(2)]
        w_vT = sb("w_vT", [P, P])
        w_fT = sb("w_fT", [P, P])
        lat_map = sb("lat_map", [P, P])
        scal = sb("scal", [P, 4])
        tanhs = sb("tanhs", [P, 2])
        cols = sb("cols", [P, 8])
        mu = sb("mu", [P, 2])
        mu_prev = sb("mu_prev", [P, 2])
        tr_sb = sb("tr_sb", [NT, NB * NB])
        tw = sb("tw", [H, NT])
        tw_max = sb("tw_max", [H, 1])
        tw_exp = sb("tw_exp", [H, NT])
        tw_sum = sb("tw_sum", [H, 1])
        tw_inv = sb("tw_inv", [H, 1])
        twT = sb("twT", [NT, H])
        lat_abs = sb("lat_abs", [NB, H])
        shift_col = sb("shift_col", [P, LEVELS, 1], BF16)
        shift_f = sb("shift_f", [P, 2])
        minus_half = sb("minus_half", [P, JB])

        q_stack = [sb(f"q_stack{n}", [QK_ROWS, H * T], BF16) for n in range(2)]
        k_stack = [sb(f"k_stack{n}", [QK_ROWS, H * T], BF16) for n in range(2)]
        i_stack = [sb(f"i_stack{n}", [BIAS_ROWS, H * T], BF16) for n in range(2)]
        j_stack = [sb(f"j_stack{n}", [BIAS_ROWS, T], BF16) for n in range(2)]
        values = [sb(f"values{n}", [P, JB, H, 32]) for n in range(2)]
        probs = sb("probs", [P, PAIR_BUFFERS, 2, T])
        w_nat = probs[:, 9].rearrange("p u (n c) -> p (u n) c", c=P)
        wo_perm = probs[:, 8, 0, 0:P]
        ones = probs[:, 8, 1, :]
        ones_rows = probs[0:H, 7].rearrange("p u i -> p (u i)").bitcast(BF16)[:, 0:LEVELS * T]
        shift_row = probs[0:1, 6].rearrange("p u i -> p (u i)").bitcast(BF16)[:, 0:LEVELS * T] \
            .rearrange("p (l i) -> p l i", l=LEVELS)

        x_nat = sb("x_nat", [P, JB, D])
        xT = sb("xT", [P, T])
        feats = sb("feats", [P, T])
        whole = sb("whole", [P, 4, T])
        parts = sb("parts", [P, 4, LEVELS, T], BF16)

        x_res = sb("x_res", [P, JB, D])
        sums_sb = sb("sums_sb", [P, 2, T])
        den_inv = sb("den_inv", [P, 2, JB, H // 2])
        attnT = sb("attnT", [P, T])
        res = sb("res", [P, JB, D])
        bn = sb("bn", [P, JB, 6])
        mean_var = sb("mean_var", [P, JB, 2])
        var_eps = sb("var_eps", [P, JB])
        rstd = sb("rstd", [P, JB])
        x1 = sb("x1", [P, JB, D])
        attn = x1
        x1T = sb("x1T", [P, 1 + T])
        gated = sb("gated", [P, JB, D])
        k_act = sb("k_act", [P, T])
        r_tanh = sb("r_tanh", [P, JB, D])
        final = sb("final", [P, JB, D])

        scratch = nc.dram_tensor("scratch", [3, LEVELS, P, T], BF16, kind="Internal").ap()
        lattice_i = nc.dram_tensor("lattice_i", [LEVELS, NB * H, T], BF16, kind="Internal").ap()
        hamming_i = nc.dram_tensor("hamming_i", [LEVELS, NB, T], BF16, kind="Internal").ap()
        ones_dram = nc.dram_tensor("ones_dram", [H, LEVELS * T], BF16, kind="Internal").ap()

        s_w, s_wf, s_w_late = sem("w_in"), sem("feature_w_in"), sem("late_w_in")
        s_beta, s_small, s_ident, s_zero = sem("beta_in"), sem("small_in"), sem("ident_made"), sem("zeroed")
        s_wT = sem("w_transposed")
        s_pool0 = sem("pool_setup")
        s_tanhs, s_twexp = sem("logit_tanhs"), sem("tw_exp_made")
        s_dve0 = sem("dve_setup")
        s_twT, s_lat, s_bound = sem("tw_transposed"), sem("lattice_product"), sem("bound_product")
        s_consts = sem("consts_made")
        s_ones_d, s_const_rows = sem("ones_in_dram"), sem("const_rows_in")

        raw_ready = sem("raw_ready")
        tanh_done = sem("tanh_done")
        bias_ready = sem("bias_ready")
        scores_done = sem("scores_done")
        exp_done = sem("exp_done")
        mask_done = sem("mask_done")
        pv_done = sem("pv_done")
        sums_read = sem("sums_read")

        dve_unit = sem("dve_unit")
        act_unit = sem("act_unit")
        dve_freed = sem("dve_freed")
        act_freed = sem("act_freed")

        x_in = sem("x_in")
        hi_done, mid_done = sem("hi_done"), sem("mid_done")
        rest_done, lo_done = sem("rest_done"), sem("lo_done")
        SCR_DMAS = [1, 1, 1, 2]
        scr_in = [sem(f"scratch_in{n}") for n in range(4)]
        STACK_DMAS = [1, LEVELS, 2, 1 + LEVELS]
        stack_in = [sem(f"stack_in{n}") for n in range(4)]
        first_qk, first_g, second_in = sem("first_qk_in"), sem("first_g_in"), sem("second_in")

        xres_in = sem("xres_in")
        den_done, attn_done = sem("den_done"), sem("attn_done")
        res_done = sem("res_done")
        bn_done, aggr_done = sem("bn_done"), sem("aggr_done")
        eps_done, rstd_done = sem("eps_done"), sem("rstd_done")
        centred = sem("centred")
        norm_done = sem("norm_done")
        kact_done = sem("kact_done")
        gate_done = sem("gate_done")
        stored = sem("stored")

        TAIL = ("first_sums_T", "den", "attn_first", "sums", "sums_T", "attn", "attn_T", "attn_T_out", "y", "res",
                "bn", "aggr", "rstd", "x1", "x1_T", "x1_T_out", "kk", "rr", "relu", "kact", "sig", "kv", "gated",
                "res2", "bn2", "aggr2", "rstd2", "final")
        tail = {name: sem(f"tail_{name}") for name in TAIL}
        HALVES = [(range(2 * n, 2 * n + 2), slice(2 * n, 2 * n + 2), slice(2 * n * P, (2 * n + 2) * P)) for n in range(2)]

        def tail_bank(stage, half):
            s = {"sums_T": 0, "attn_T": 1, "y": 2, "x1_T": 0, "kk": 1, "rr": 2, "kv": 0}[stage]
            return raw[:, s, 512 * half:512 * (half + 1)]

        passed = sem("passed")

        block = ctx.enter_context(nc.Block())

        def side_place(b, use):
            if isinstance(b, int) and b < 0 and use in ("q", "k"):
                u = "qk".index(use)
                return raw[:, 2, 512 * u:512 * (u + 1)]
            return side_bank[:]

        def pair_units(t):
            quad, p = divmod(t, PAIRS_PER_QUAD)
            if p < 2:
                return [[(4 * quad + r, 0, 0, T)] for r in (2 * p, 2 * p + 1)]
            if p < 4:
                return [[(4 * quad + r, 1, 0, 3 * P), (4 * quad + r, 3, 3 * P, P)] for r in (2 * p - 4, 2 * p - 3)]
            return [[(4 * quad + r, 2, (r % 2) * 2 * P, 2 * P) for r in (2 * u, 2 * u + 1)] for u in range(2)]

        def last_of_group(t):
            quad, p = divmod(t, PAIRS_PER_QUAD)
            return quad * PAIRS_PER_QUAD + LAST_OF_GROUP[p]

        def pair_probs(t):
            return probs[:, t % PAIR_BUFFERS]

        def lagged(b, t, lag):
            return (b, t - lag) if t >= lag else (b - 1, t - lag + PAIRS)

        def stand_alone(eng):
            eng.sem_inc(passed, 1)

        @block.sync
        def _(sp):
            sp.dma_start(x_nat[:], x[0].rearrange("(n p) c -> p n c", p=P)).then_inc(x_in, 16)
            sp.dma_start(w_nat[:, 0:3, :], qkv_w.rearrange("(t p) c -> p t c", p=P)).then_inc(s_w, 16)
            sp.wait_ge(s_zero, 1)
            for at, w in ((0, q6_w), (HEX_J, hex_w)):
                sp.dma_start(w_nat[at:at + LEVELS * NB, 7, :],
                             w.unsqueeze(0).broadcast_to([LEVELS, NB, D])).then_inc(s_wf, 16)
            sp.dma_start(w_nat[HEX_I:HEX_I + NB, 7, :], hex_w).then_inc(s_wf, 16)
            sp.dma_start(scal[:, 3:4], beta.partition_broadcast(P)).then_inc(s_beta, 16)
            for n, s in enumerate((lam_logit, scale_logit, alpha)):
                sp.dma_start(scal[:, n:n + 1], s.partition_broadcast(P)).then_inc(s_small, 16)
            sp.dma_start(tw[:], transform_weights).then_inc(s_small, 16)
            sp.dma_start(tr_sb[:], transforms.rearrange("t d e -> t (d e)")).then_inc(s_small, 16)
            sp.wait_ge(s_dve0, DVE0_ONES)
            sp.dma_start(ones_dram, ones_rows).then_inc(s_ones_d, 16)
            for n, w in enumerate((out_w, w_r, w_k, w_v)):
                sp.dma_start(w_nat[:, 3 + n, :], w).then_inc(s_w_late, 16)
            sp.dma_start(mu[:, 0:1], mu_r.rearrange("(p a) -> p a", a=1)).then_inc(s_w_late, 16)
            sp.dma_start(mu[:, 1:2], mu_k.rearrange("(p a) -> p a", a=1)).then_inc(s_w_late, 16)
            sp.wait_ge(s_ones_d, 16)
            for n in range(2):
                sp.dma_start(i_stack[n][SHIFT_ROW:BIAS_ROWS, :],
                             ones_dram.rearrange("h (l i) -> l h i", l=LEVELS)).then_inc(s_const_rows, 16)

            def to_dram(kind):
                done = scr_in[kind]
                if kind == G:
                    sp.dma_start(lattice_i.rearrange("l p i -> p l i"), parts[0:NB * H, G]).then_inc(done, 16)
                    sp.dma_start(hamming_i.rearrange("l p i -> p l i"),
                                 parts[HEX_I:HEX_I + NB, G]).then_inc(done, 16)
                else:
                    sp.dma_start(scratch[kind].rearrange("l p i -> p l i"), parts[:, kind]).then_inc(done, 16)

            def load_stack(kind, par, ready, heads=(0, H)):
                first, n = heads[0] * T, (heads[1] - heads[0]) * T
                if kind == Q:
                    src = scratch[Q].rearrange("l (d h) i -> (l d) (h i)", h=H)[:, first:first + n]
                    sp.dma_start(q_stack[par][:, first:first + n],
                                 src.unsqueeze(0).broadcast_to([LEVELS, LEVELS * HD, n])).then_inc(ready, 16)
                for level in range(LEVELS):
                    r, ham = level * LEVELS * HD, LAT_ROWS + level * LEVELS * NB
                    if kind == K:
                        src = scratch[K, level].rearrange("(d h) i -> d (h i)", h=H)[:, first:first + n]
                        sp.dma_start(k_stack[par][r:r + LEVELS * HD, first:first + n],
                                     src.unsqueeze(0).broadcast_to([LEVELS, HD, n])).then_inc(ready, 16)
                    if kind == G:
                        src = hamming_i.rearrange("l e i -> (l e) i").unsqueeze(1)
                        sp.dma_start(i_stack[par][ham:ham + LEVELS * NB, first:first + n].rearrange(
                                         "e (h i) -> e h i", i=T),
                                     src.broadcast_to([LEVELS * NB, n // T, T])).then_inc(ready, 16)
                if kind == J:
                    for at, row in ((0, 0), (LAT_ROWS, HEX_J)):
                        sp.dma_start(j_stack[par][at:at + LAT_ROWS, :],
                                     scratch[J][:, row:row + LEVELS * NB, :]).then_inc(ready, 16)
                if kind == G:
                    src = lattice_i.rearrange("l (e h) i -> (l e) (h i)", h=H)[:, first:first + n]
                    sp.dma_start(i_stack[par][0:LAT_ROWS, first:first + n],
                                 src.unsqueeze(0).broadcast_to([LEVELS, LEVELS * NB, n])).then_inc(ready, 16)

            def stacks(n, par):
                for kind in (Q, K, J, G):
                    sp.wait_ge(lo_done, 4 * n + kind + 1)
                    stand_alone(sp)
                    sp.wait_ge(stack_in[kind], 16 * STACK_DMAS[kind] * n)
                    to_dram(kind)
                if not (isinstance(n, int) and n < 2):
                    sp.wait_ge(raw_ready, PAIRS * (n - 1))
                    stand_alone(sp)
                    sp.wait_ge(bias_ready, PAIRS * (n - 1))
                for kind in (Q, K, J, G):
                    sp.wait_ge(scr_in[kind], 16 * SCR_DMAS[kind] * (n + 1))
                    load_stack(kind, par, stack_in[kind])

            def first_stacks():
                for kind in (Q, K):
                    sp.wait_ge(lo_done, kind + 1)
                    to_dram(kind)
                for kind in (Q, K):
                    sp.wait_ge(scr_in[kind], 16)
                    load_stack(kind, 0, first_qk, (0, 4))
                for kind in (J, G):
                    sp.wait_ge(lo_done, kind + 1)
                    to_dram(kind)
                sp.wait_ge(scr_in[J], 16)
                load_stack(J, 0, stack_in[J])
                sp.wait_ge(scr_in[G], 16 * SCR_DMAS[G])
                load_stack(G, 0, first_g, (0, 4))
                sp.wait_ge(s_consts, 1)
                for n in range(2):
                    sp.dma_start(j_stack[n][SHIFT_ROW:BIAS_ROWS, :], shift_row).then_inc(s_const_rows, 16)
                for kind in (Q, K, G):
                    load_stack(kind, 0, second_in, (4, 8))
                for kind in (Q, K, G):
                    load_stack(kind, 0, stack_in[kind], (8, H))

            def period(b, par, post, prep):
                if post:
                    sp.wait_ge(dve_freed, side_units.start(b, False))
                    stand_alone(sp)
                    sp.dma_start(x_res[:], x[b - 1].rearrange("(n p) c -> p n c", p=P)).then_inc(xres_in, 16)
                if prep:
                    stacks(b + 1, 1 - par)
                if post and not prep:
                    sp.wait_ge(dve_freed, side_units.through(b, "y"))
                    sp.dma_start(x_res[:], x[b].rearrange("(n p) c -> p n c", p=P)).then_inc(xres_in, 16)
                if post:
                    store(b - 1)

            def store(n):
                sp.wait_ge(norm_done, 2 * (n + 1))
                stand_alone(sp)
                sp.dma_start(out[n].rearrange("(n p) c -> p n c", p=P), final[:]).then_inc(stored, 16)
                sp.wait_ge(stored, 16 * (n + 1))
                stand_alone(sp)

            first_stacks()
            period(0, 0, False, True)
            with sp.Fori(1, B - 2, 2) as i:
                period(i, 1, True, True)
                period(i + 1, 0, True, True)
            period(B - 1, 1, True, False)
            for half, (_, bs, _) in enumerate(HALVES):
                sp.wait_ge(tail["final"], half + 1)
                sp.dma_start(out[B - 1].rearrange("(n p) c -> p n c", p=P)[:, bs], final[:, bs]).then_inc(stored, 16)
            sp.wait_ge(stored, 16 * (B + 1))

        @block.tensor
        def _(pe):
            def mm(o, lhsT, rhs, start=True, stop=True, **kw):
                return nc.tensor.matmul(o, lhsT, rhs, start=start, stop=stop, **kw)

            def scores(b, par, t):
                first = isinstance(b, int) and b == 0
                if first and t == 0:
                    pe.wait_ge(first_qk, 16 * (1 + LEVELS))
                elif first and t == PAIRS_PER_QUAD:
                    pe.wait_ge(second_in, 16 * (1 + LEVELS + 1 + LEVELS))
                elif t == (2 * PAIRS_PER_QUAD if first else 0):
                    pe.wait_ge(stack_in[Q], 16 * STACK_DMAS[Q] * (b + 1))
                    pe.wait_ge(stack_in[K], 16 * STACK_DMAS[K] * (b + 1))
                if first and t < PSUM_PAIRS:
                    pe.wait_ge(s_dve0, DVE0_END if t else DVE0_WEIGHTS)
                else:
                    before = t - PSUM_PAIRS if t >= PSUM_PAIRS else \
                        max(o for o in range(PAIRS) if o % PSUM_PAIRS == t) - PAIRS
                    pe.wait_ge(scores_done, PAIRS * b + before + 1)
                for u, bank in enumerate(pair_units(t)):
                    for h, jb, at, n in bank:
                        last = mm(raw[:, t % PSUM_PAIRS, 512 * u + at:512 * u + at + n],
                                  k_stack[par][:, h * T + jb * P:h * T + (jb + 1) * P],
                                  q_stack[par][:, h * T + jb * P:(h + 1) * T])
                last.then_inc(raw_ready, 1)

            def biases(b, par, t):
                first = isinstance(b, int) and b == 0
                if t == 0:
                    pe.wait_ge(stack_in[J], 16 * STACK_DMAS[J] * (b + 1))
                if first and t == 0:
                    pe.wait_ge(first_g, 16 * (1 + LEVELS))
                    pe.wait_ge(s_const_rows, 16 * 4)
                elif t == (2 * PAIRS_PER_QUAD if first else 0):
                    pe.wait_ge(stack_in[G], 16 * STACK_DMAS[G] * (b + 1))
                pe.wait_ge(tanh_done, PAIRS * b + t + 1)
                for u, bank in enumerate(pair_units(t)):
                    for h, jb, at, n in bank:
                        last = mm(raw[:, t % PSUM_PAIRS, 512 * u + at:512 * u + at + n],
                                  j_stack[par][:, jb * P:(jb + 1) * P],
                                  i_stack[par][:, h * T + jb * P:(h + 1) * T])
                last.then_inc(bias_ready, 1)

            def weighted(b, par, t):
                quad, p = divmod(t, PAIRS_PER_QUAD)
                k, s = divmod(quad, 2)
                pe.wait_ge(mask_done, PAIRS * b + last_of_group(t) + 1)
                if t == 0:
                    pe.wait_ge(mid_done, 4 * (b + 1))
                if t == PAIRS // 2 or (t == 0 and not (isinstance(b, int) and b == 0)):
                    pe.wait_ge(sums_read, 2 * b + k)
                first_pair = last_of_group(t) - (1 if p < 4 else 0)

                def head(r, a, z):
                    return pair_probs(first_pair + (r // 2 if p < 4 else 0))[:, r % 2 if p < 4 else r // 2, a:z]

                jb, first, cols_of = [
                    (0, 0, lambda r: head(r, 0, T // 2)), (0, T // 2, lambda r: head(r, T // 2, T)),
                    (1, P, lambda r: head(r, 0, 3 * P)), (3, 3 * P, lambda r: head(r, 3 * P, T)),
                    (2, 2 * P, lambda r: head(r, (r % 2) * 2 * P, (r % 2 + 1) * 2 * P))][p]
                for r in range(4):
                    rhs = cols_of(r)
                    last = mm(sums[32 * r:32 * r + 32, first:first + rhs.shape[-1]],
                              values[par][:, jb, 4 * quad + r, :], rhs, start=(s == 0 and p == 0),
                              stop=(s == 1 and p == PAIRS_PER_QUAD - 1), skip_group_check=True)
                last.then_inc(pv_done, 1)

            def four(o, lhsT, rhs):
                for n in range(JB):
                    last = mm(o[:, n * P:(n + 1) * P], lhsT[:, n * P:(n + 1) * P], rhs)
                return last

            def four_transposes(o, src):
                for n in range(JB):
                    last = nc.tensor.transpose(o[:, n * P:(n + 1) * P], src(n), ident[:])
                return last

            def side(b, use):
                nx, pv = b + 1, b - 1
                o = side_place(b, use)
                before = side_units.before(b, use)
                if use == "F" and isinstance(b, int) and b < 0:
                    pe.wait_ge(dve_freed, side_units.through(b, "xT"))
                elif before:
                    pe.wait_ge(act_freed if before[0] else dve_freed, before[1])
                done = act_unit if use in ACT_UNITS else dve_unit
                if use == "xT":
                    pe.wait_ge(x_in, 16 * (nx + 1))
                    last = four_transposes(o, lambda n: x_nat[:, n, :])
                elif use in ("q", "k"):
                    pe.wait_ge(dve_freed, side_units.through(b, "xT"))
                    last = mm(o, wqT[:] if use == "q" else wkT[:], xT[:])
                elif use == "F":
                    last = mm(o, w_fT[:], xT[:])
                elif use == "v":
                    last = four(o, xT, wvT[:])
                elif use == "G":
                    pe.wait_ge(act_freed, side_units.through(b, "F"))
                    last = mm(o, lat_map[:], feats[:])
                elif use in ("oT0", "oT1"):
                    k = int(use[-1])
                    pe.wait_ge(sums_read, 2 * pv + 1 + k)
                    last = four_transposes(o, lambda n: sums_sb[:, k, n * P:(n + 1) * P])
                elif use == "aT":
                    pe.wait_ge(dve_freed, side_units.through(b, "oT1"))
                    last = four_transposes(o, lambda n: attn[:, n, :])
                elif use == "y":
                    pe.wait_ge(dve_freed, side_units.through(b, "aT"))
                    last = four(o, attnT, woT[:])
                elif use == "x1T":
                    pe.wait_ge(norm_done, 2 * pv + 1)
                    last = four_transposes(o, lambda n: x1[:, n, :])
                elif use == "kk":
                    pe.wait_ge(dve_freed, side_units.through(b, "x1T"))
                    mm(o, w_k_mix[0][:], x1T[:, 1:1 + T], stop=False)
                    last = mm(o, w_k_mix[1][:], x1T[:, 0:T], start=False)
                elif use == "rr":
                    pe.wait_ge(dve_freed, side_units.through(b, "x1T"))
                    for n in range(JB):
                        mm(o[:, n * P:(n + 1) * P], x1T[:, 1 + n * P:1 + (n + 1) * P], w_r_mix[0][:], stop=False)
                        last = mm(o[:, n * P:(n + 1) * P], x1T[:, n * P:(n + 1) * P], w_r_mix[1][:], start=False)
                elif use == "kv":
                    pe.wait_ge(kact_done, pv + 1)
                    last = four(o, k_act, w_vT[:])
                last.then_inc(done, 1)

            def values_of(b, par, step):
                for t in range(PAIRS):
                    if VALUES_STEPS[t] == step:
                        weighted(b, par, t)

            def period(b, par, post, prep):
                for t in range(PAIRS):
                    def ahead():
                        if t + 1 < PAIRS:
                            scores(b, par, t + 1)
                        elif prep:
                            scores(b + 1, 1 - par, 0)

                    if t >= BIAS_LAG or post:
                        batch, pair = lagged(b, t, BIAS_LAG)
                        biases(batch, par if t >= BIAS_LAG else 1 - par, pair)
                    if t in AHEAD_FIRST:
                        ahead()
                    for use in (PREP_UNITS.get(t, []) if prep else []) + (POST_UNITS.get(t, []) if post else []):
                        side(b, use)
                    if post:
                        values_of(b - 1, 1 - par, t + PAIRS)
                    values_of(b, par, t)
                    if t not in AHEAD_FIRST:
                        ahead()

            def transposed(out, names):
                for n, src in enumerate(names):
                    last = nc.tensor.transpose(out[:, n * P:(n + 1) * P], src, ident[:])
                return last

            pe.wait_ge(s_ident, 1)
            side(-1, "xT")
            pe.wait_ge(s_w, 16)
            pe.wait_ge(s_wf, 16 * 3)
            transposed(raw[:, 0], [w_nat[:, n, :] for n in (0, 1, 7, 2)]).then_inc(s_wT, 1)
            pe.wait_ge(s_dve0, DVE0_WEIGHTS)
            for use in ("q", "k", "F"):
                side(-1, use)
            pe.wait_ge(s_dve0, DVE0_TW)
            nc.tensor.transpose(raw[0:NT, 1, 0:H], tw[:], ident[0:H, 0:H]).then_inc(s_twT, 1)
            pe.wait_ge(s_dve0, DVE0_TWT)
            for e in range(NB):
                last = mm(raw[0:NB, 1, 512 + e * H:512 + (e + 1) * H],
                          tr_sb[:].rearrange("t (d e) -> t d e", e=NB)[:, :, e], twT[:])
            last.then_inc(s_lat, 1)
            pe.wait_ge(s_dve0, DVE0_LATTICE)
            side(-1, "G")
            pe.wait_ge(s_dve0, DVE0_ABS)
            mm(raw[:, 1, 0:H], ones[0:NB, 0:P], lat_abs[:]).then_inc(s_bound, 1)
            side(-1, "v")
            scores(0, 0, 0)
            pe.wait_ge(s_w_late, 16 * 6)
            pe.wait_ge(s_zero, 2)
            transposed(raw[:, 2], [wo_perm] + [w_nat[:, n, :] for n in (4, 5, 6)]).then_inc(s_wT, 1)
            period(0, 0, False, True)
            with pe.Fori(1, B - 2, 2) as i:
                period(i, 1, True, True)
                period(i + 1, 0, True, True)
            period(B - 1, 1, True, False)
            for t in range(PAIRS - BIAS_LAG, PAIRS):
                biases(B - 1, 1, t)

            def transposes(o, src, blocks):
                for n in blocks:
                    last = nc.tensor.transpose(o[:, n * P:(n + 1) * P], src(n), ident[:])
                return last

            pe.wait_ge(sums_read, 2 * B - 1)
            pe.wait_ge(dve_freed, side_units.start(B, False))
            transposes(side_bank, lambda n: sums_sb[:, 0, n * P:(n + 1) * P],
                       range(JB)).then_inc(tail["first_sums_T"], 1)
            for step in range(PAIRS, VALUES_STEPS[-1] + 1):
                values_of(B - 1, 1, step)
            pe.wait_ge(scores_done, PAIRS * B)
            for half, (blocks, _, _) in enumerate(HALVES):
                pe.wait_ge(tail["sums"], half + 1)
                transposes(tail_bank("sums_T", half), lambda n: sums_sb[:, 1, n * P:(n + 1) * P],
                           blocks).then_inc(tail["sums_T"], 1)
            for half, (blocks, _, _) in enumerate(HALVES):
                pe.wait_ge(tail["attn_first"], 1)
                pe.wait_ge(tail["attn"], half + 1)
                transposes(tail_bank("attn_T", half), lambda n: attn[:, n, :], blocks).then_inc(tail["attn_T"], 1)
            for half, (blocks, _, _) in enumerate(HALVES):
                pe.wait_ge(tail["attn_T_out"], half + 1)
                for n in blocks:
                    last = mm(tail_bank("y", half)[:, n * P:(n + 1) * P], attnT[:, n * P:(n + 1) * P], woT[:])
                last.then_inc(tail["y"], 1)
            for half, (blocks, _, _) in enumerate(HALVES):
                pe.wait_ge(tail["x1"], half + 1)
                transposes(tail_bank("x1_T", half), lambda n: x1[:, n, :], blocks).then_inc(tail["x1_T"], 1)
            for half, (blocks, _, cs) in enumerate(HALVES):
                pe.wait_ge(tail["x1_T_out"], half + 1)
                now, prev = slice(cs.start + 1, cs.stop + 1), cs
                o = tail_bank("kk", half)[:, cs]
                mm(o, w_k_mix[0][:], x1T[:, now], stop=False)
                mm(o, w_k_mix[1][:], x1T[:, prev], start=False).then_inc(tail["kk"], 1)
                for n in blocks:
                    o = tail_bank("rr", half)[:, n * P:(n + 1) * P]
                    mm(o, x1T[:, 1 + n * P:1 + (n + 1) * P], w_r_mix[0][:], stop=False)
                    last = mm(o, x1T[:, n * P:(n + 1) * P], w_r_mix[1][:], start=False)
                last.then_inc(tail["rr"], 1)
            for half, (blocks, _, _) in enumerate(HALVES):
                pe.wait_ge(tail["kact"], half + 1)
                for n in blocks:
                    last = mm(tail_bank("kv", half)[:, n * P:(n + 1) * P], k_act[:, n * P:(n + 1) * P], w_vT[:])
                last.then_inc(tail["kv"], 1)

        @block.scalar
        def _(act):
            def tanh(b, t):
                act.wait_ge(raw_ready, PAIRS * b + t + 1)
                if not (isinstance(b, int) and b == 0 and t < PAIR_BUFFERS):
                    act.wait_ge(pv_done, PAIRS * b + last_of_group(t) - PAIR_BUFFERS + 1)
                nc.scalar.activation(pair_probs(t), raw[:, t % PSUM_PAIRS, :].rearrange("p (u i) -> p u i", u=2),
                                     ACT.Tanh).then_inc(tanh_done, 1)

            def exp(b, t):
                act.wait_ge(scores_done, PAIRS * b + t + 1)
                nc.scalar.activation(pair_probs(t), pair_probs(t), ACT.Exp).then_inc(exp_done, 1)

            def side(b, use):
                nx, pv = b + 1, b - 1
                early = isinstance(b, int) and b < 0
                o = side_place(b, use)
                act.wait_ge(act_unit, side_units.through(b, use))
                if use == "F":
                    if not early:
                        act.wait_ge(lo_done, 4 * nx)
                    ins = nc.scalar.activation(feats[:], o, ACT.Tanh)
                elif use == "kk":
                    ins = nc.scalar.activation(k_act[:], o, ACT.Relu)
                elif use == "rr":
                    ins = nc.scalar.activation(r_tanh[:].rearrange("p n c -> p (n c)"), o, ACT.Tanh, scale=0.5)
                ins.then_inc(act_freed, 1)
                if use == "kk":
                    act.wait_ge(act_freed, side_units.through(b, "kk"))
                    nc.scalar.activation(k_act[:], k_act[:], ACT.Square).then_inc(kact_done, 1)

            def sides(b, t, post, prep):
                for use in (PREP_UNITS.get(t, []) if prep else []) + (POST_UNITS.get(t, []) if post else []):
                    if use in ACT_UNITS:
                        side(b, use)

            def period(b, par, post, prep):
                if prep:
                    act.wait_ge(dve_unit, side_units.start(b, False))
                    act.dma_start(x_nat[:], x[b + 1].rearrange("(n p) c -> p n c", p=P)).then_inc(x_in, 16)
                for t in range(PAIRS):
                    tanh(b, t)
                    if t >= EXP_LAG or post:
                        exp(*lagged(b, t, EXP_LAG))
                    sides(b, t, post, prep)

            act.wait_ge(s_small, 16 * 5)
            nc.scalar.activation(tanhs[:], scal[:, 0:2], ACT.Tanh, scale=0.5).then_inc(s_tanhs, 1)
            act.wait_ge(s_dve0, DVE0_TWMAX)
            nc.scalar.activation(tw_exp[:], tw[:], ACT.Exp, bias=tw_max[:], scale=1.0 / TEMP,
                                 accum_out=tw_sum[:]).then_inc(s_twexp, 1)
            side(-1, "F")
            act.wait_ge(s_dve0, DVE0_SHIFT)
            nc.scalar.activation(shift_row, shift_col[0:1].broadcast_to([1, LEVELS, T]),
                                 ACT.Copy).then_inc(s_consts, 1)
            period(0, 0, False, True)
            with act.Fori(1, B - 2, 2) as i:
                period(i, 1, True, True)
                period(i + 1, 0, True, True)
            period(B - 1, 1, True, False)
            for t in range(PAIRS - EXP_LAG, PAIRS):
                exp(B - 1, t)

            for half, (_, _, cs) in enumerate(HALVES):
                act.wait_ge(tail["attn_T"], half + 1)
                nc.scalar.activation(attnT[:, cs], tail_bank("attn_T", half)[:, cs], ACT.Copy).then_inc(tail["attn_T_out"], 1)
            for half, (_, _, cs) in enumerate(HALVES):
                act.wait_ge(tail["x1_T"], half + 1)
                nc.scalar.activation(x1T[:, cs.start + 1:cs.stop + 1], tail_bank("x1_T", half)[:, cs],
                                     ACT.Copy).then_inc(tail["x1_T_out"], 1)
            for half, (_, bs, cs) in enumerate(HALVES):
                act.wait_ge(tail["kk"], half + 1)
                nc.scalar.activation(k_act[:, cs], tail_bank("kk", half)[:, cs],
                                     ACT.Relu).then_inc(tail["relu"], 1)
                act.wait_ge(tail["relu"], half + 1)
                nc.scalar.activation(k_act[:, cs], k_act[:, cs], ACT.Square).then_inc(tail["kact"], 1)
                act.wait_ge(tail["rr"], half + 1)
                nc.scalar.activation(r_tanh[:, bs, :], tail_bank("rr", half)[:, cs].rearrange("p (n c) -> p n c", c=D), ACT.Tanh,
                                     scale=0.5).then_inc(tail["sig"], 1)

        @block.gpsimd
        def _(pool):
            nc.gpsimd.memset(ident[:], 0.0).then_inc(s_pool0, 1)
            pool.wait_ge(s_pool0, 1)
            nc.gpsimd.affine_select(out=ident[:], in_=ident[:], compare_op=ALU.not_equal, fill=1.0, base=0,
                                    pattern=[[-1, P]], channel_multiplier=1).then_inc(s_ident, 1)
            for n in range(2):
                nc.gpsimd.memset(values[n][:], 0.0).then_inc(s_pool0, 1)
            pool.wait_ge(s_pool0, 3)
            for n in range(2):
                for s in range(2):
                    v = values[n][:].rearrange("p j (k s r) m -> p (j k) s r m", k=2, s=2)
                    nc.gpsimd.memset(v[:, :, s, :, NP * s + HD], 1.0).then_inc(s_pool0, 1)

            def mask(b, t):
                v, p = pair_probs(t), t % PAIRS_PER_QUAD
                if p < 4:
                    blocks = [v[:, :, 0:P]] + ([v[:, :, 3 * P:T]] if p >= 2 else [])
                else:
                    blocks = [v.rearrange("p u (r i) -> p (u r) i", r=2)[:, :, 0:P]]
                pool.wait_ge(exp_done, PAIRS * b + t + 1)
                stand_alone(pool)
                for v in blocks:
                    last = nc.gpsimd.affine_select(out=v, in_=v, compare_op=ALU.is_ge, fill=0.0, base=0,
                                                   pattern=[[0, v.shape[1]], [1, P]], channel_multiplier=-1)
                last.then_inc(mask_done, 1)

            def rest(n, kind):
                pool.wait_ge(hi_done, 4 * n + kind + 1)
                nc.gpsimd.tensor_tensor(whole[:, kind, :], feats[:] if kind == J else whole[:, kind, :],
                                        parts[:, kind, 0, :], ALU.subtract).then_inc(rest_done, 1)

            def lo(n, kind):
                pool.wait_ge(mid_done, 4 * n + kind + 1)
                nc.gpsimd.tensor_tensor(parts[:, kind, 2, :], whole[:, kind, :], parts[:, kind, 1, :],
                                        ALU.subtract).then_inc(lo_done, 1)

            def inv_std(n, which):
                m = 2 * n + which
                pool.wait_ge(aggr_done, JB * (m + 1))
                stand_alone(pool)
                nc.gpsimd.tensor_scalar(var_eps[:], mean_var[:, :, 1], LN_EPS, None, ALU.add).then_inc(eps_done, 1)
                pool.wait_ge(eps_done, m + 1)
                nc.gpsimd.tensor_tensor(rstd[:], var_eps[:], minus_half[:], ALU.pow).then_inc(rstd_done, 1)

            def norm(n, which):
                dst, m = x1 if which == 0 else final, 2 * n + which
                nc.gpsimd.tensor_tensor(dst[:], res[:], mean_var[:, :, 0:1].broadcast_to([P, JB, D]),
                                        ALU.subtract).then_inc(centred, 1)
                pool.wait_ge(rstd_done, m + 1)
                pool.wait_ge(centred, m + 1)
                nc.gpsimd.tensor_tensor(dst[:], dst[:], rstd[:].unsqueeze(2).broadcast_to([P, JB, D]),
                                        ALU.mult).then_inc(norm_done, 1)

            def gated_residual(n):
                pool.wait_ge(dve_freed, side_units.through(n + 1, "kv"))
                nc.gpsimd.tensor_tensor(res[:], gated[:], x1[:], ALU.add).then_inc(gate_done, 1)

            PREP = {3: [(rest, Q), (rest, K)], 4: [(lo, Q)], 6: [(rest, J)], 7: [(lo, K)], 8: [(rest, G)],
                    9: [(lo, J), (lo, G)]}
            POST = {10: [(inv_std, 0)], 11: [(norm, 0)], 18: [(gated_residual,)], 19: [(inv_std, 1), (norm, 1)]}

            def period(b, par, post, prep):
                for t in range(PAIRS):
                    if t >= EXP_LAG or post:
                        mask(*lagged(b, t, EXP_LAG))
                    for stage, *a in PREP.get(t, []) if prep else []:
                        stage(b + 1, *a)
                    for stage, *a in POST.get(t, []) if post and (prep or t < PAIRS - 1) else []:
                        stage(b - 1, *a)

            for kind in (K, J):
                rest(0, kind)
                lo(0, kind)
            period(0, 0, False, True)
            with pool.Fori(1, B - 2, 2) as i:
                period(i, 1, True, True)
                period(i + 1, 0, True, True)
            period(B - 1, 1, True, False)
            for t in range(PAIRS - EXP_LAG, PAIRS):
                mask(B - 1, t)
            inv_std(B - 2, 1)
            norm(B - 2, 1)

            for after, done, m in (("aggr", "rstd", 2 * B - 2), ("aggr2", "rstd2", 2 * B)):
                for half, (_, bs, _) in enumerate(HALVES):
                    pool.wait_ge(tail[after], 2 * (half + 1))
                    nc.gpsimd.tensor_scalar(var_eps[:, bs], mean_var[:, bs, 1], LN_EPS, None,
                                            ALU.add).then_inc(eps_done, 1)
                    pool.wait_ge(eps_done, m + half + 1)
                    nc.gpsimd.tensor_tensor(rstd[:, bs], var_eps[:, bs], minus_half[:, bs],
                                            ALU.pow).then_inc(tail[done], 1)

        @block.vector
        def _(dve):
            made = [0]

            def link(ins):
                made[0] += 1
                ins.then_inc(s_dve0, 1)
                dve.wait_ge(s_dve0, made[0])

            def mark(value):
                assert made[0] == value, (made[0], value)

            v = nc.vector

            def main(b, t):
                dve.wait_ge(bias_ready, PAIRS * b + t + 1)
                dve.wait_ge(tanh_done, PAIRS * b + t + 1)
                o = pair_probs(t)
                v.scalar_tensor_tensor(out=o, in0=o, scalar=scal[:, 2:3],
                                       in1=raw[:, t % PSUM_PAIRS, :].rearrange("p (u i) -> p u i", u=2),
                                       op0=ALU.mult, op1=ALU.add).then_inc(scores_done, 1)

            def unit(b, use):
                dve.wait_ge(dve_unit, side_units.through(b, use))
                return side_place(b, use)

            def x_out(n):
                v.tensor_copy(xT[:], unit(n - 1, "xT")).then_inc(dve_freed, 1)

            def projected(n, kind):
                o = unit(n - 1, "qk"[kind])
                if not (isinstance(n, int) and n == 0):
                    dve.wait_ge(lo_done, 4 * (n - 1) + kind + 1)
                if kind == Q:
                    v.tensor_scalar(whole[:, Q, :], o, cols[:, 2:3], None, ALU.mult).then_inc(dve_freed, 1)
                else:
                    v.tensor_copy(whole[:, K, :], o).then_inc(dve_freed, 1)

            def hi(n, kind):
                if kind in (Q, K):
                    dve.wait_ge(dve_freed, side_units.through(n - 1, "qk"[kind]))
                elif kind == G:
                    dve.wait_ge(dve_freed, side_units.through(n - 1, "G"))
                else:
                    dve.wait_ge(act_freed, side_units.through(n - 1, "F"))
                if not (isinstance(n, int) and n == 0):
                    dve.wait_ge(scr_in[kind], 16 * SCR_DMAS[kind] * n)
                v.tensor_copy(parts[:, kind, 0, :], feats[:] if kind == J else whole[:, kind, :]).then_inc(hi_done, 1)

            def mid(n, kind):
                dve.wait_ge(rest_done, 4 * n + kind + 1)
                v.tensor_copy(parts[:, kind, 1, :], whole[:, kind, :]).then_inc(mid_done, 1)

            def values_in(n):
                o = unit(n - 1, "v")
                if isinstance(n, int) and n < 2:
                    dve.wait_ge(s_pool0, 3 + 4)
                else:
                    dve.wait_ge(pv_done, PAIRS * (n - 1))
                for s in range(2):
                    dst = values[parity[0]][:].rearrange("p j (k s r) m -> p (j k) s r m", k=2, s=2)
                    src = o.rearrange("p (j s r d) -> p j s r d", s=2, r=4, d=HD)
                    last = v.tensor_copy(dst[:, :, s, :, NP * s:NP * s + HD], src[:, :, s])
                last.then_inc(dve_freed, 1)

            def features_i(n):
                v.tensor_copy(whole[:, G, :], unit(n - 1, "G")).then_inc(dve_freed, 1)

            def sums_out(n, k):
                dve.wait_ge(pv_done, PAIRS * n + (k + 1) * PAIRS // 2)
                v.tensor_copy(sums_sb[:, k, :], sums[:]).then_inc(sums_read, 1)

            def normalise(n, k):
                o = unit(n + 1, f"oT{k}").rearrange("p (n q m) -> p n q m", n=JB, m=NP)
                v.reciprocal(den_inv[:, k], o[:, :, :, HD]).then_inc(den_done, 1)
                dve.wait_ge(den_done, 2 * n + k + 1)
                dst = attn[:].rearrange("p n (k q d) -> p n k q d", k=2, d=HD)[:, :, k]
                v.tensor_tensor(dst, o[:, :, :, 0:HD],
                                den_inv[:, k].unsqueeze(3).broadcast_to([P, JB, H // 2, HD]),
                                ALU.mult).then_inc(dve_freed, 1)

            def attn_out(n):
                v.tensor_copy(attnT[:], unit(n + 1, "aT")).then_inc(dve_freed, 1)

            def stats(n, which, half):
                if which == 0:
                    dve.wait_ge(dve_freed, side_units.through(n + 1, "y"))
                else:
                    dve.wait_ge(gate_done, n + 1)
                for blk in (2 * half, 2 * half + 1):
                    v.bn_stats(bn[:, blk, :], res[:, blk, :]).then_inc(bn_done, 1)

            def moments(n, which):
                dve.wait_ge(bn_done, JB * (2 * n + which + 1))
                stand_alone(dve)
                for blk in range(JB):
                    v.bn_aggr(mean_var[:, blk, :], bn[:, blk, :]).then_inc(aggr_done, 1)

            def residual(n):
                o = unit(n + 1, "y").rearrange("p (n c) -> p n c", n=JB)
                dve.wait_ge(xres_in, 16 * (n + 1))
                v.tensor_tensor(res[:], o, x_res[:], ALU.add).then_inc(dve_freed, 1)

            def x1_out(n):
                v.tensor_copy(x1T[:, 1:1 + T], unit(n + 1, "x1T")).then_inc(dve_freed, 1)

            def gate(n):
                o = unit(n + 1, "kv").rearrange("p (n c) -> p n c", n=JB)
                dve.wait_ge(act_freed, side_units.through(n + 1, "rr"))
                v.scalar_tensor_tensor(out=gated[:], in0=r_tanh[:], scalar=1.0, in1=o, op0=ALU.add,
                                       op1=ALU.mult).then_inc(dve_freed, 1)

            PREP = {0: [(x_out,)], 2: [(projected, Q)], 3: [(projected, K), (hi, Q), (hi, K)], 4: [(mid, Q)],
                    5: [(hi, J)], 7: [(features_i,), (hi, G), (mid, K), (mid, J)],
                    9: [(values_in,), (mid, G)]}
            POST = {1: [(normalise, 0)], 6: [(normalise, 1)], 8: [(attn_out,)],
                    10: [(residual,), (stats, 0, 0), (stats, 0, 1), (moments, 0)], 14: [(x1_out,)],
                    18: [(gate,)], 19: [(stats, 1, 0), (stats, 1, 1), (moments, 1)]}

            def period(b, par, post, prep):
                parity[0] = 1 - par
                for t in range(PAIRS):
                    if t == VALUES_STEPS[-1] - PAIRS and post:
                        sums_out(b - 1, 1)
                    if t == VALUES_STEPS[PAIRS // 2 - 1]:
                        sums_out(b, 0)
                    if t >= BIAS_LAG or post:
                        main(*lagged(b, t, BIAS_LAG))
                    for stage, *a in PREP.get(t, []) if prep else []:
                        stage(b + 1, *a)
                    for stage, *a in POST.get(t, []) if post else []:
                        stage(b - 1, *a)

            def rest_here(kind):
                dve.wait_ge(hi_done, kind + 1)
                if kind:
                    dve.wait_ge(rest_done, kind)
                w = whole[:, kind, :]
                v.tensor_tensor(w, w, parts[:, kind, 0, :], ALU.subtract).then_inc(rest_done, 1)

            def lo_here(kind):
                dve.wait_ge(mid_done, kind + 1)
                if kind:
                    dve.wait_ge(lo_done, kind)
                v.tensor_tensor(parts[:, kind, 2, :], whole[:, kind, :], parts[:, kind, 1, :],
                                ALU.subtract).then_inc(lo_done, 1)

            parity = [0]
            v.memset(w_nat[:, 7, :], 0.0).then_inc(s_zero, 1)
            link(v.memset(ones_rows, 1.0))
            mark(DVE0_ONES)
            link(v.memset(minus_half[:], -0.5))
            link(v.memset(x1T[:, 0:1], 0.0))
            link(v.memset(lat_map[:], 0.0))
            link(v.memset(ones, 1.0))
            x_out(0)
            dve.wait_ge(s_beta, 16)
            link(v.reciprocal(cols[:, 2:3], scal[:, 3:4]))
            mark(DVE0_BETA)
            dve.wait_ge(s_wT, 1)
            for n, w in enumerate((wqT, wkT)):
                link(v.tensor_copy(w[:].rearrange("p (d h) -> p d h", h=H),
                                   raw[:, 0, n * P:(n + 1) * P].rearrange("p (h d) -> p d h", h=H)))
            link(v.tensor_copy(w_fT[:], raw[:, 0, 2 * P:3 * P]))
            link(v.tensor_copy(wvT[:], raw[:, 0, 3 * P:4 * P]))
            mark(DVE0_WEIGHTS)
            dve.wait_ge(s_small, 16 * 5)
            link(v.tensor_reduce(tw_sum[:], tw[:], AX.X, ALU.max))
            link(v.tensor_scalar(tw_max[:], tw_sum[:], -1.0 / TEMP, None, ALU.mult))
            mark(DVE0_TWMAX)
            projected(0, Q)
            hi(0, Q)
            rest_here(Q)
            mid(0, Q)
            projected(0, K)
            hi(0, K)
            lo_here(Q)
            dve.wait_ge(s_tanhs, 1)
            link(v.tensor_scalar(cols[:, 0:1], tanhs[:, 0:1], 0.25, 0.25, ALU.mult, ALU.add))
            link(v.tensor_scalar(cols[:, 1:2], tanhs[:, 1:2], 1.0 / NB, 1.0 / NB, ALU.mult, ALU.add))
            dve.wait_ge(s_ident, 1)
            link(v.tensor_scalar(lat_map[HEX_I:P, HEX_I:P], ident[HEX_I:P, HEX_I:P], cols[HEX_I:P, 0:1], None,
                                 ALU.mult))
            dve.wait_ge(s_twexp, 1)
            link(v.reciprocal(tw_inv[:], tw_sum[:]))
            link(v.tensor_scalar(tw[:], tw_exp[:], tw_inv[:], None, ALU.mult))
            mark(DVE0_TW)
            mid(0, K)
            dve.wait_ge(s_twT, 1)
            link(v.tensor_copy(twT[:], raw[0:NT, 1, 0:H]))
            mark(DVE0_TWT)
            hi(0, J)
            dve.wait_ge(s_lat, 1)
            link(v.tensor_scalar(lat_map[0:NB, 0:NB * H], raw[0:NB, 1, 512:512 + NB * H], cols[0:NB, 1:2], None,
                                 ALU.mult))
            mark(DVE0_LATTICE)
            link(v.tensor_reduce(lat_abs[:], lat_map[0:NB, 0:NB * H].rearrange("d (e h) -> d h e", h=H), AX.X,
                                 ALU.add, apply_absolute_value=True))
            mark(DVE0_ABS)
            link(v.scalar_tensor_tensor(out=cols[:, 3:4], in0=scal[:, 2:3], scalar=-1.0, in1=scal[:, 2:3],
                                        op0=ALU.mult, op1=ALU.max))
            link(v.scalar_tensor_tensor(out=cols[:, 4:5], in0=cols[:, 0:1], scalar=float(NB), in1=cols[:, 3:4],
                                        op0=ALU.mult, op1=ALU.add))
            features_i(0)
            hi(0, G)
            mid(0, J)
            rest_here(G)
            mid(0, G)
            lo_here(G)
            dve.wait_ge(s_bound, 1)
            link(v.tensor_reduce(cols[:, 5:6], raw[:, 1, 0:H], AX.X, ALU.max))
            link(v.scalar_tensor_tensor(out=cols[:, 6:7], in0=cols[:, 4:5], scalar=-1.0, in1=cols[:, 5:6],
                                        op0=ALU.mult, op1=ALU.subtract))
            link(v.tensor_scalar(cols[:, 6:7], cols[:, 6:7], SAFE_SCORE, 0.0, ALU.add, ALU.min))
            link(v.tensor_copy(shift_col[:, 0], cols[:, 6:7]))
            link(v.tensor_tensor(shift_f[:, 0:1], cols[:, 6:7], shift_col[:, 0], ALU.subtract))
            link(v.tensor_copy(shift_col[:, 1], shift_f[:, 0:1]))
            link(v.tensor_tensor(shift_f[:, 1:2], shift_f[:, 0:1], shift_col[:, 1], ALU.subtract))
            link(v.tensor_copy(shift_col[:, 2], shift_f[:, 1:2]))
            mark(DVE0_SHIFT)
            values_in(0)
            dve.wait_ge(s_w_late, 16 * 6)
            for k in range(2):
                for s in range(2):
                    src = w_nat[:, 3, :].rearrange("p (k s r d) -> p k s r d", k=2, s=2, r=4)[:, k, s]
                    dst = wo_perm.rearrange("p (k r s d) -> p k r s d", k=2, s=2, r=4)[:, k, :, s]
                    last = v.tensor_copy(dst, src)
            last.then_inc(s_zero, 1)
            link(v.tensor_scalar(mu_prev[:], mu[:], -1.0, 1.0, ALU.mult, ALU.add))
            dve.wait_ge(s_wT, 2)
            link(v.tensor_copy(woT[:], raw[:, 2, 0:P]))
            for n, w in enumerate((w_r_mix, w_k_mix)):
                src = raw[:, 2, (n + 1) * P:(n + 2) * P]
                link(v.tensor_scalar(w[0][:], src, mu[:, n:n + 1], None, ALU.mult))
                link(v.tensor_scalar(w[1][:], src, mu_prev[:, n:n + 1], None, ALU.mult))
            link(v.tensor_scalar(w_vT[:], raw[:, 2, 3 * P:4 * P], 0.5, None, ALU.mult))
            mark(DVE0_END)

            period(0, 0, False, True)
            with dve.Fori(1, B - 2, 2) as i:
                period(i, 1, True, True)
                period(i + 1, 0, True, True)
            period(B - 1, 1, True, False)
            for t in range(PAIRS - BIAS_LAG, PAIRS):
                main(B - 1, t)

            def split_heads(o):
                return o.rearrange("p (n q m) -> p n q m", n=JB, m=NP)

            def divide(k, bs, o, made, done):
                v.reciprocal(den_inv[:, k, bs], o[:, bs, :, HD]).then_inc(tail["den"], 1)
                dve.wait_ge(tail["den"], made)
                dst = attn[:].rearrange("p n (k q d) -> p n k q d", k=2, d=HD)[:, bs, k]
                v.tensor_tensor(dst, o[:, bs, :, 0:HD],
                                den_inv[:, k, bs].unsqueeze(3).broadcast_to([P, bs.stop - bs.start, H // 2, HD]),
                                ALU.mult).then_inc(tail[done], 1)

            def tail_stats(half, blocks, res_name, bn_name, aggr_name):
                dve.wait_ge(tail[res_name], half + 1)
                for n in blocks:
                    v.bn_stats(bn[:, n, :], res[:, n, :]).then_inc(tail[bn_name], 1)
                dve.wait_ge(tail[bn_name], 2 * (half + 1))
                for n in blocks:
                    v.bn_aggr(mean_var[:, n, :], bn[:, n, :]).then_inc(tail[aggr_name], 1)

            def tail_norm(half, blocks, rstd_name, dst, done):
                dve.wait_ge(tail[rstd_name], half + 1)
                for n in blocks:
                    last = v.tensor_scalar(dst[:, n, :], res[:, n, :], mean_var[:, n, 0:1], rstd[:, n:n + 1],
                                           ALU.subtract, ALU.mult)
                last.then_inc(tail[done], 1)

            dve.wait_ge(tail["first_sums_T"], 1)
            divide(0, slice(0, JB), split_heads(side_bank[:]), 1, "attn_first")
            dve.wait_ge(pv_done, PAIRS * B)
            for half, (_, _, cs) in enumerate(HALVES):
                v.tensor_copy(sums_sb[:, 1, cs], sums[:, cs]).then_inc(tail["sums"], 1)
            for half, (_, bs, _) in enumerate(HALVES):
                dve.wait_ge(tail["sums_T"], half + 1)
                divide(1, bs, split_heads(tail_bank("sums_T", half)), half + 2, "attn")
            dve.wait_ge(xres_in, 16 * B)
            dve.wait_ge(norm_done, 2 * (B - 1))
            for half, (blocks, bs, cs) in enumerate(HALVES):
                dve.wait_ge(tail["y"], half + 1)
                y = tail_bank("y", half).rearrange("p (n c) -> p n c", c=D)
                v.tensor_tensor(res[:, bs], y[:, bs], x_res[:, bs], ALU.add).then_inc(tail["res"], 1)
                tail_stats(half, blocks, "res", "bn", "aggr")
            for half, (blocks, _, _) in enumerate(HALVES):
                tail_norm(half, blocks, "rstd", x1, "x1")
            for half, (blocks, bs, cs) in enumerate(HALVES):
                dve.wait_ge(tail["sig"], half + 1)
                dve.wait_ge(tail["kv"], half + 1)
                kv = tail_bank("kv", half).rearrange("p (n c) -> p n c", c=D)
                v.scalar_tensor_tensor(out=gated[:, bs], in0=r_tanh[:, bs], scalar=1.0, in1=kv[:, bs], op0=ALU.add,
                                       op1=ALU.mult).then_inc(tail["gated"], 1)
                dve.wait_ge(tail["gated"], half + 1)
                v.tensor_tensor(res[:, bs], gated[:, bs], x1[:, bs], ALU.add).then_inc(tail["res2"], 1)
                tail_stats(half, blocks, "res2", "bn2", "aggr2")
            dve.wait_ge(stored, 16 * (B - 1))
            for half, (blocks, _, _) in enumerate(HALVES):
                tail_norm(half, blocks, "rstd2", final, "final")


INPUTS = ["L0_attn_x", "L0_attn_qkv_w", "L0_attn_out_w", "L0_attn_hex_w", "L0_attn_hamming_lambda_logit",
          "L0_attn_q6_w", "L0_attn_transforms", "L0_attn_transform_weights", "L0_attn_scale_logit",
          "L0_attn_sips_alpha", "L0_attn_sips_beta", "L0_ffn_W_r", "L0_ffn_W_k", "L0_ffn_W_v", "L0_ffn_mu_r",
          "L0_ffn_mu_k"]


def kernel(**inputs):
    import numpy as np
    import concourse.bacc as bacc
    from concourse import mybir as types
    from concourse.bass_utils import run_bass_kernel_spmd

    nc = bacc.Bacc("TRN2", target_bir_lowering=False, num_devices=1,
                   dynamic_dma_scratch_size=8192)
    arrays, args = {}, []
    for name in INPUTS:
        a = np.ascontiguousarray(inputs[name])
        a = a.reshape(a.shape or (1,))
        arrays[f"in_{name}"] = a
        args.append(nc.dram_tensor(f"in_{name}", a.shape, types.dt.from_np(a.dtype), kind="ExternalInput").ap())
    shape = inputs["L0_attn_x"].shape
    out = nc.dram_tensor("out", shape, types.dt.float32, kind="ExternalOutput").ap()
    build(nc, *args, out)
    return run_bass_kernel_spmd(nc, [arrays], core_ids=[0]).results[0]["out"]
```
